# Optimizing a Trainium2 kernel written in Bass

```python
import numpy as np
import jax
import jax.numpy as jnp

def _softmax(x, axis=-1):
    return jax.nn.softmax(x, axis=axis)

def _gelu(x):
    return jax.nn.gelu(x, approximate=True)

def _silu(x):
    return jax.nn.silu(x)

def _sigmoid(x):
    return jax.nn.sigmoid(x)

def _layernorm(x, axis=-1, eps=1e-05):
    m = jnp.mean(x, axis=axis, keepdims=True)
    v = jnp.var(x, axis=axis, keepdims=True)
    return (x - m) / jnp.sqrt(v + eps)

def _scatter_add(tgt, idx, src, axis=0):
    return tgt.at[idx].add(src)

def _segment_sum(src, seg, n):
    return jax.ops.segment_sum(src, seg, n)
kernel_name = 'mk_adaln_d1_jaxref_r8_333ef6'

def setup_inputs(seed: int=0):
    np.random.seed(seed)
    _w = jnp.asarray

    def _L0_attn_setup():
        import jax, jax.numpy as jnp
        import numpy as np
        D = 128
        N = 64
        EPS = 1e-06
        key = jax.random.key(seed)
        ks = jax.random.split(key, 10)
        sD = 1.0 / np.sqrt(D)
        sN = 1.0 / np.sqrt(N)
        x = jax.random.normal(ks[0], (8, 512, D), dtype=jnp.float32)
        A_log = jax.random.normal(ks[1], (N,), dtype=jnp.float32)
        WB = jax.random.uniform(ks[2], (N, D), jnp.float32, -sD, sD)
        bB = jax.random.uniform(ks[3], (N,), jnp.float32, -sD, sD)
        WC = jax.random.uniform(ks[4], (N, D), jnp.float32, -sD, sD)
        bC = jax.random.uniform(ks[5], (N,), jnp.float32, -sD, sD)
        Wd = jax.random.uniform(ks[6], (1, D), jnp.float32, -sD, sD)
        bd = jax.random.uniform(ks[7], (1,), jnp.float32, -sD, sD)
        Wo = jax.random.uniform(ks[8], (D, N), jnp.float32, -sN, sN)
        bo = jax.random.uniform(ks[9], (D,), jnp.float32, -sN, sN)
        return {'x': x, 'A_log': A_log, 'WB': WB, 'bB': bB, 'WC': WC, 'bC': bC, 'Wd': Wd, 'bd': bd, 'Wo': Wo, 'bo': bo}
    _L0_attn_in = _L0_attn_setup()

    def _L0_ffn_setup():
        import jax, jax.numpy as jnp
        import numpy as np
        TOP_K = 8
        key = jax.random.key(seed)
        ks = jax.random.split(key, 6)
        B, S, D, F, E = (2, 128, 128, 64, 64)
        x = jax.random.normal(ks[0], (B, S, D), dtype=jnp.float32)
        centroids = jax.random.normal(ks[1], (E, D), dtype=jnp.float32) * 0.05
        expert_biases = jnp.zeros((E,), dtype=jnp.float32)
        Ws_up = jax.random.normal(ks[2], (D, F), dtype=jnp.float32) / np.sqrt(D)
        Ws_down = jax.random.normal(ks[3], (F, D), dtype=jnp.float32) / np.sqrt(F)
        W_up = jax.random.normal(ks[4], (E, D, F), dtype=jnp.float32) / np.sqrt(D)
        W_down = jax.random.normal(ks[5], (E, F, D), dtype=jnp.float32) / np.sqrt(F)
        return {'x': x, 'centroids': centroids, 'expert_biases': expert_biases, 'Ws_up': Ws_up, 'Ws_down': Ws_down, 'W_up': W_up, 'W_down': W_down}
    _L0_ffn_in = _L0_ffn_setup()
    _L0_c = _w((lambda *s: np.random.randn(*s).astype(np.float32) * 0.05)(16, 128))
    _L0_wmod = _w((lambda *s: np.random.randn(*s).astype(np.float32) * 0.05)(128, 6 * 128) * 128 ** (-0.5))
    _d = {'L0_attn_x': _L0_attn_in['x'], 'L0_attn_A_log': _L0_attn_in['A_log'], 'L0_attn_WB': _L0_attn_in['WB'], 'L0_attn_bB': _L0_attn_in['bB'], 'L0_attn_WC': _L0_attn_in['WC'], 'L0_attn_bC': _L0_attn_in['bC'], 'L0_attn_Wd': _L0_attn_in['Wd'], 'L0_attn_bd': _L0_attn_in['bd'], 'L0_attn_Wo': _L0_attn_in['Wo'], 'L0_attn_bo': _L0_attn_in['bo'], 'L0_ffn_centroids': _L0_ffn_in['centroids'], 'L0_ffn_expert_biases': _L0_ffn_in['expert_biases'], 'L0_ffn_Ws_up': _L0_ffn_in['Ws_up'], 'L0_ffn_Ws_down': _L0_ffn_in['Ws_down'], 'L0_ffn_W_up': _L0_ffn_in['W_up'], 'L0_ffn_W_down': _L0_ffn_in['W_down'], 'L0_c': _L0_c, 'L0_wmod': _L0_wmod}
    _x0 = _d['L0_attn_x']
    _d['L0_attn_x'] = jax.random.normal(jax.random.fold_in(jax.random.key(seed), 1), (16, 256, 128), dtype=_x0.dtype)
    del _x0
    return _d

def reference(L0_attn_x, L0_attn_A_log, L0_attn_WB, L0_attn_bB, L0_attn_WC, L0_attn_bC, L0_attn_Wd, L0_attn_bd, L0_attn_Wo, L0_attn_bo, L0_ffn_centroids, L0_ffn_expert_biases, L0_ffn_Ws_up, L0_ffn_Ws_down, L0_ffn_W_up, L0_ffn_W_down, L0_c, L0_wmod):

    def _L0_attn_ref(x, A_log, WB, bB, WC, bC, Wd, bd, Wo, bo):
        import jax, jax.numpy as jnp
        import numpy as np
        D = 128
        N = 64
        EPS = 1e-06
        A = -jax.nn.softplus(A_log)
        B_t = jnp.einsum('bld,nd->bln', x, WB) + bB
        _C_proj = jnp.einsum('bld,nd->bln', x, WC) + bC
        Delta = jax.nn.softplus(jnp.einsum('bld,nd->bln', x, Wd) + bd)
        dA = jnp.exp(A * Delta)
        dB = (dA - 1.0) / (A + EPS) * B_t
        conv = jnp.cumprod(dA, axis=1)
        ones = jnp.ones_like(dA[:, :1, :])
        Ct = jnp.concatenate([ones, conv[:, :-1, :]], axis=1)
        z = dB / (Ct + EPS)
        s = jnp.cumsum(z, axis=1)
        X_state = Ct * s
        Y = jnp.einsum('bln,dn->bld', Ct * X_state, Wo) + bo
        return Y

    def _L0_ffn_ref(x, centroids, expert_biases, Ws_up, Ws_down, W_up, W_down):
        import jax, jax.numpy as jnp
        import numpy as np
        TOP_K = 8
        B, S, D = x.shape
        E = centroids.shape[0]
        T = B * S
        xf = x.reshape(T, D)
        shared = jax.nn.silu(xf @ Ws_up) @ Ws_down
        aff = xf @ centroids.T
        biased = aff + expert_biases
        _, idx = jax.lax.top_k(biased, TOP_K)
        sel = jnp.take_along_axis(aff, idx, axis=1)
        w = jax.nn.sigmoid(sel)
        w = w / (jnp.sum(w, axis=-1, keepdims=True) + 1e-08)
        cw = jnp.zeros((T, E), dtype=x.dtype).at[jnp.arange(T)[:, None], idx].add(w)
        h = jax.nn.silu(jnp.einsum('td,edf->etf', xf, W_up))
        y = jnp.einsum('etf,efd->etd', h, W_down)
        routed = jnp.einsum('etd,te->td', y, cw)
        return (shared + routed).reshape(B, S, D)
    x = L0_attn_x
    mod = (_silu(L0_c) @ L0_wmod).reshape(L0_c.shape[0], 6, 1, -1)
    sa, ca, ga, sb, cb, gb = (mod[:, 0], mod[:, 1], mod[:, 2], mod[:, 3], mod[:, 4], mod[:, 5])
    ga = (2 * (ga >= 0) - 1) * jnp.maximum(jnp.abs(ga), 0.25)
    gb = (2 * (gb >= 0) - 1) * jnp.maximum(jnp.abs(gb), 0.25)
    h = _layernorm(x, axis=-1) * (1 + ca) + sa
    x = x + ga * _L0_attn_ref(h, L0_attn_A_log, L0_attn_WB, L0_attn_bB, L0_attn_WC, L0_attn_bC, L0_attn_Wd, L0_attn_bd, L0_attn_Wo, L0_attn_bo)
    h = _layernorm(x, axis=-1) * (1 + cb) + sb
    x = x + gb * _L0_ffn_ref(h, L0_ffn_centroids, L0_ffn_expert_biases, L0_ffn_Ws_up, L0_ffn_Ws_down, L0_ffn_W_up, L0_ffn_W_down)
    return x

_drawn_inputs = setup_inputs


def setup_inputs(seed=0):
    import zlib

    import numpy as np

    out = dict(_drawn_inputs(seed))
    spreads = {'L0_ffn_expert_biases': (0.0, 2.0)}
    factors = {'L0_attn_A_log': 8.0,
     'L0_attn_WB': 6.518,
     'L0_attn_bB': 8.0,
     'L0_attn_Wd': 8.0,
     'L0_attn_Wo': 6.28,
     'L0_attn_bo': 64.0,
     'L0_ffn_centroids': 31.96,
     'L0_ffn_Ws_up': 8.0,
     'L0_ffn_Ws_down': 8.0,
     'L0_ffn_W_up': 35.369,
     'L0_ffn_W_down': 29.61}
    for name, (base, spread) in spreads.items():
        noise = np.random.default_rng([zlib.crc32(name.encode()), seed]).standard_normal(out[name].shape)
        drawn = base * np.exp(spread * noise) if base else spread * noise
        out[name] = jnp.asarray(drawn.astype(out[name].dtype))
    for name, factor in factors.items():
        out[name] = (out[name] * factor).astype(out[name].dtype)
    return out
```

```python
import concourse.bass as bass
from concourse import mybir
from contextlib import ExitStack


def adaln_ssm_moe_kernel(nc, x, A_log, WB, bB, Wd, bd, Wo, bo, centroids, expert_biases,
                         Ws_up, Ws_down, W_up, W_down, c, wmod, out):
    fp32 = mybir.dt.float32
    r32 = mybir.dt.float32r
    i32 = mybir.dt.int32
    ALU = mybir.AluOpType
    ACT = mybir.ActivationFunctionType
    AX = mybir.AxisListType

    P = 128
    BATCH, S, D = x.shape
    N = A_log.shape[0]
    E, _, F = W_up.shape
    GT = 2 * S
    G = BATCH * S // GT
    TL = GT // P
    NC = E * F // P + 1
    NR = NC - 1
    RING = 3
    LAG = 3
    TOPK = 8
    LN_EPS, SSM_EPS, SUM_EPS = 1e-5, 1e-6, 1e-8
    U_POLY = -0.1
    LOWEST = -3.0e38
    EULER = 2.718281828459045
    RSQRT_GUESS, RSQRT_STEPS = float(0x5F3759DF), 4
    SA, CA, GA, SB, CB, GB, BOGA = range(7)
    PIECE = 8
    NP = NR // PIECE
    STAGES = 4
    assert D == P and 2 * N == P and 2 * F == P and NC % RING == 0 and NR % 2 == 0 and NR % PIECE == 0

    x_v = x.rearrange("b s d -> (b s) d").rearrange("(g t p) d -> g p t d", t=TL, p=P)
    out_v = out.rearrange("b s d -> (b s) d").rearrange("(g t p) d -> g p t d", t=TL, p=P)
    up_v = W_up.rearrange("e d f -> d e f")
    down_v = W_down.rearrange("e f d -> (e f) d").rearrange("(c p) d -> p c d", p=P)

    ctx = ExitStack()
    with ctx:
        def sb(name, shape, dt=fp32):
            return ctx.enter_context(nc.sbuf_tensor(name, shape, dt))

        def sem(name):
            return ctx.enter_context(nc.semaphore(name))

        x_sb = sb("x_sb", [P, G, TL, D])
        ident = sb("ident", [P, P])
        both = sb("both", [P, E])
        sel = sb("sel", [P, E, F], r32)
        stage = sb("stage", [P, STAGES, PIECE * P])
        shared_raw = sb("shared_raw", [P, 2, P])
        up_hi = sb("up_hi", [P, NC, P], r32)
        up_lo = sb("up_lo", [P, NC, P], r32)
        down_hi = sb("down_hi", [P, NC, P], r32)
        down_lo = sb("down_lo", [P, NC, P], r32)
        WB_sb = sb("WB_sb", [N, D])
        Wd_sb = sb("Wd_sb", [D, 1])
        Wo_sb = sb("Wo_sb", [P, 2, N])
        cent_sb = sb("cent_sb", [E, D])
        WB_T = sb("WB_T", [D, N])
        Wo_T = sb("Wo_T", [P, D])
        cent_T = sb("cent_T", [D, E])
        bB_sb = sb("bB_sb", [P, 1])
        bd_sb = sb("bd_sb", [P, 1])
        bo_sb = sb("bo_sb", [D, 1])
        bias_sb = sb("bias_sb", [P, E])
        A_sb = sb("A_sb", [P, 1])
        rA = sb("rA", [P, 1])
        pad = sb("pad", [P, 1])
        minus_one = sb("minus_one", [P, 1])
        wk = sb("wk", [P, 16])
        wki = sb("wki", [P, 1], i32)
        c_sb = sb("c_sb", [BATCH, D])
        cs_sb = sb("cs_sb", [BATCH, D])
        cs_T = sb("cs_T", [D, BATCH])
        wmod_sb = sb("wmod_sb", [D, 6 * D])
        mod = sb("mod", [D, 7, BATCH])
        sgn = sb("sgn", [D, 2, BATCH])
        stats = sb("stats", [P, TL, 6])
        mv = sb("mv", [P, TL, 2])
        rs = sb("rs", [P, 6, TL])
        xn = sb("xn", [P, TL, D])
        h1T = sb("h1T", [D, GT])
        sp = sb("sp", [P, 8, TL])
        delta_b = sb("delta_b", [P, TL, N])
        u_sb = sb("u_sb", [P, S])
        uc_sb = sb("uc_sb", [P, S])
        su_sb = sb("su_sb", [P, S])
        p_sb = sb("p_sb", [P, S])
        mask_u = sb("mask_u", [P, S], i32)
        dA = sb("dA", [P, S])
        Ct = sb("Ct", [P, S])
        dB = sb("dB", [P, S])
        zeros = sb("zeros", [P, S])
        y_sb = sb("y_sb", [P, S])
        uT = sb("uT", [D, GT])
        h2T = sb("h2T", [D, GT])
        aff = sb("aff", [P, TL, E])
        biased = sb("biased", [P, TL, E])
        left = sb("left", [P, TL, E])
        top = sb("top", [P, TL, TOPK])
        chosen = sb("chosen", [P, TL, E])
        az = sb("az", [P, TL, E])
        sz = sb("sz", [P, TL, E])
        ez = sb("ez", [P, TL, E])
        wsum = sb("wsum", [P, TL])
        cw_hl = sb("cw_hl", [P, TL, 2, E], r32)
        h2_hi = sb("h2_hi", [D, GT], r32)
        h2_lo = sb("h2_lo", [D, GT], r32)
        cw_T = sb("cw_T", [2 * E, GT], r32)
        s_ring = sb("s_ring", [P, RING, GT])
        g_ring = sb("g_ring", [P, RING, GT])
        g_hi = sb("g_hi", [P, RING, GT], r32)
        g_lo = sb("g_lo", [P, RING, GT], r32)
        fT = sb("fT", [D, GT])
        out_sb = sb("out_sb", [P, TL, D])

        def bank(name):
            return ctx.enter_context(nc.psum_tensor(name, [P, GT], fp32))

        up_ps = [bank(f"up_ps{i}") for i in range(RING)]
        cw_ps = [bank(f"cw_ps{i}") for i in range(2)]
        down_ps = bank("down_ps")
        T_ps = bank("T_ps")
        Q_ps = bank("Q_ps")

        x_in = [sem(f"x_in{i}") for i in range(G)]
        c_in, wmod_in, vec_in, WB_in, Wo_in, cent_in = (sem(n) for n in (
            "c_in", "wmod_in", "vec_in", "WB_in", "Wo_in", "cent_in"))
        shared_in = sem("shared_in")
        piece_in = [sem(f"piece_in{i}") for i in range(2 * NP)]
        out_done = sem("out_done")
        ident_done, pool_own, act_own, dve_own = (sem(n) for n in ("ident_done", "pool_own", "act_own", "dve_own"))
        shared_clear, both_done, sel_done = (sem(n) for n in ("shared_clear", "both_done", "sel_done"))
        cs_done, csT_ps, csT_done, mod_ps, mod_done = (sem(n) for n in (
            "cs_done", "csT_ps", "csT_done", "mod_ps", "mod_done"))
        wT_ps, wT_done = sem("wT_ps"), sem("wT_done")
        w_hi, w_lo = sem("w_hi"), sem("w_lo")
        names = ("xn1_done", "xn1_ps", "h1_done", "b_ps", "spz_done", "sps_done", "delta_done", "delta_ps",
                 "uc_done", "su_done", "y_done", "y_ps", "u_done", "u_ps", "xn2_done", "xn2_ps", "h2_done",
                 "aff_ps", "az_done", "sz_done", "cw_done", "cwT_ps", "h2hi_done", "h2lo_done", "cwT_done",
                 "f_done", "f_ps", "out_ready")
        (xn1_done, xn1_ps, h1_done, b_ps, spz_done, sps_done, delta_done, delta_ps,
         uc_done, su_done, y_done, y_ps, u_done, u_ps, xn2_done, xn2_ps, h2_done,
         aff_ps, az_done, sz_done, cw_done, cwT_ps, h2hi_done, h2lo_done, cwT_done,
         f_done, f_ps, out_ready) = (sem(n) for n in names)
        up_done, bc_done, s_done, g_done, hi_done, lo_done, down_done = (sem(n) for n in (
            "up_done", "bc_done", "s_done", "g_done", "hi_done", "lo_done", "down_done"))

        def need(eng, s, value):
            if not isinstance(value, int) or value > 0:
                eng.wait_ge(s, value)

        def chunks(g, ch):
            return g * NC + (ch + 1)

        def routed(g, ch):
            return g * NR + ch

        def up_of(g, j):
            return (g, j + LAG) if j + LAG < NC else (g + 1, j + LAG - NC)

        block = ctx.enter_context(nc.Block())

        @block.sync
        def _(sync):
            sync.dma_start(c_sb[:], c).then_inc(c_in, 16)
            sync.dma_start(x_sb[:, 0], x_v[0]).then_inc(x_in[0], 16)
            sync.dma_start(wmod_sb[:], wmod).then_inc(wmod_in, 16)
            sync.dma_start(WB_sb[:], WB).then_inc(WB_in, 16)
            for h in range(2):
                sync.dma_start(wk[h * N:(h + 1) * N, 0:1], A_log.rearrange("(n o) -> n o", o=1)).then_inc(vec_in, 16)
                sync.dma_start(bB_sb[h * N:(h + 1) * N, :], bB.rearrange("(n o) -> n o", o=1)).then_inc(vec_in, 16)
                sync.dma_start(Wo_sb[:, h, :], Wo).then_inc(Wo_in, 16)
            sync.dma_start(Wd_sb[:], Wd.rearrange("o d -> d o")).then_inc(vec_in, 16)
            sync.dma_start(bo_sb[:], bo.rearrange("(d o) -> d o", o=1)).then_inc(vec_in, 16)
            sync.dma_start(bd_sb[:], bd.rearrange("(o n) -> o n", o=1).broadcast_to([P, 1])).then_inc(vec_in, 16)
            sync.dma_start(bias_sb[:], expert_biases.rearrange("(o n) -> o n", o=1).broadcast_to([P, E])).then_inc(vec_in, 16)
            sync.dma_start(cent_sb[:], centroids).then_inc(cent_in, 16)
            sync.wait_ge(shared_clear, 1)
            sync.dma_start(shared_raw[:, 0, 0:F], Ws_up).then_inc(shared_in, 16)
            sync.dma_start(shared_raw[0:F, 1, :], Ws_down).then_inc(shared_in, 16)
            for k in range(2 * NP):
                i = k // 2
                if k >= STAGES:
                    sync.wait_ge(w_lo, k - STAGES + 2)
                if k % 2 == 0:
                    for e0 in range(0, 2 * PIECE, PIECE):
                        sync.dma_start(
                            stage[:, k % STAGES, e0 * F:(e0 + PIECE) * F].rearrange("d (e f) -> d e f", f=F),
                            up_v[:, i * 2 * PIECE + e0:i * 2 * PIECE + e0 + PIECE, :]).then_inc(piece_in[k], 16)
                else:
                    for c0 in range(0, PIECE, PIECE // 2):
                        sync.dma_start(
                            stage[:, k % STAGES, c0 * P:(c0 + PIECE // 2) * P].rearrange("p (c d) -> p c d", d=D),
                            down_v[:, i * PIECE + c0:i * PIECE + c0 + PIECE // 2, :]).then_inc(piece_in[k], 16)
                if k >= 1 and k < G:
                    sync.dma_start(x_sb[:, k], x_v[k]).then_inc(x_in[k], 16)
            with sync.Fori(0, G) as g:
                sync.wait_ge(out_ready, g + 1)
                sync.dma_start(out_v[bass.ds(g, 1)].rearrange("o p t d -> (o p) t d"), out_sb[:]).then_inc(out_done, 16)
            sync.wait_ge(out_done, 16 * G)

        @block.gpsimd
        def _(pool):
            nc.gpsimd.memset(shared_raw[:], 0.0).then_inc(shared_clear, 1)
            nc.gpsimd.memset(ident[:], 0.0).then_inc(pool_own, 1)
            pool.wait_ge(pool_own, 1)
            nc.gpsimd.affine_select(out=ident[:], in_=ident[:], compare_op=ALU.not_equal, fill=1.0, base=0,
                                    pattern=[[-1, P]], channel_multiplier=1).then_inc(ident_done, 1)
            nc.gpsimd.memset(minus_one[:], -1.0)
            nc.gpsimd.memset(zeros[:], 0.0).then_inc(ident_done, 1)

            for k in range(2 * NP + 1):
                pool.wait_ge(w_hi, 2 * (k + 1) if k == 0 else k + 2)
                if k == 0:
                    nc.gpsimd.tensor_tensor(up_lo[:, 0, :], shared_raw[:, 0, :], up_hi[:, 0, :].bitcast(fp32),
                                            ALU.subtract)
                    nc.gpsimd.tensor_tensor(down_lo[:, 0, :], shared_raw[:, 1, :], down_hi[:, 0, :].bitcast(fp32),
                                            ALU.subtract).then_inc(w_lo, 1)
                else:
                    lo, hi = (up_lo, up_hi) if (k - 1) % 2 == 0 else (down_lo, down_hi)
                    c0 = 1 + (k - 1) // 2 * PIECE
                    nc.gpsimd.tensor_tensor(
                        lo[:, c0:c0 + PIECE, :],
                        stage[:, (k - 1) % STAGES].rearrange("p (c m) -> p c m", m=P),
                        hi[:, c0:c0 + PIECE, :].bitcast(fp32), ALU.subtract).then_inc(w_lo, 1)

            def lo_part(g, ch):
                pool.wait_ge(hi_done, chunks(g, ch))
                nc.gpsimd.tensor_tensor(g_lo[:, ch % RING], g_ring[:, ch % RING],
                                        g_hi[:, ch % RING].bitcast(fp32), ALU.subtract).then_inc(lo_done, 1)

            lo_part(0, 0)
            for ch in range(1, LAG):
                lo_part(0, ch)
            with pool.Fori(0, G - 1) as g:
                for j in range(NC):
                    lo_part(*up_of(g, j))
            for j in range(NC - LAG):
                lo_part(*up_of(G - 1, j))

        @block.scalar
        def _(act):
            def mod_of(row, g, half):
                return mod[:, row, bass.ds(2 * g + half, 1)]

            def modulate(dst, src, scale_row, bias_row, g):
                for half in range(2):
                    cols = slice(half * S, (half + 1) * S)
                    src_ps = src[half]
                    if bias_row is None:
                        last = nc.scalar.activation(dst[:, cols], src_ps[:, cols], ACT.Copy,
                                                    scale=mod_of(scale_row, g, half))
                    else:
                        last = nc.scalar.activation(dst[:, cols], src_ps[:, cols], ACT.Identity,
                                                    scale=mod_of(scale_row, g, half), bias=mod_of(bias_row, g, half))
                return last

            def norm1(g):
                act.wait_ge(xn1_ps, g + 1)
                modulate(h1T, (T_ps, T_ps), CA, SA, g).then_inc(h1_done, 1)

            def step_size(g):
                act.wait_ge(spz_done, g + 1)
                nc.scalar.activation(sp[:, 2], sp[:, 1], ACT.Silu, scale=-1.0).then_inc(sps_done, 1)

            def decay(g):
                act.wait_ge(uc_done, g + 1)
                nc.scalar.activation(su_sb[:], uc_sb[:], ACT.Silu).then_inc(su_done, 1)

            def gate1(g):
                act.wait_ge(y_ps, g + 1)
                modulate(uT, (T_ps, Q_ps), GA, BOGA, g).then_inc(u_done, 1)

            def norm2(g):
                act.wait_ge(xn2_ps, g + 1)
                modulate(h2T, (T_ps, T_ps), CB, SB, g).then_inc(h2_done, 1)

            def router(g):
                act.wait_ge(az_done, g + 1)
                nc.scalar.activation(sz[:], az[:], ACT.Silu, scale=-1.0, bias=minus_one[:, 0:1]).then_inc(sz_done, 1)

            def hand_over(g):
                act.wait_ge(h2_done, g + 1)
                need(act, up_done, chunks(g - 1, NC - 1))
                nc.scalar.copy(h2_hi[:], h2T[:]).then_inc(h2hi_done, 1)
                act.wait_ge(cwT_ps, g + 1)
                need(act, bc_done, routed(g - 1, NR))
                nc.scalar.copy(cw_T[:], T_ps[:]).then_inc(cwT_done, 1)

            def silu_part(g, ch):
                act.wait_ge(up_done, chunks(g, ch))
                if ch == 0:
                    need(act, lo_done, chunks(g - 1, NC - RING))
                    nc.scalar.activation(g_ring[:, 0], up_ps[0][:], ACT.Silu).then_inc(s_done, 1)
                else:
                    need(act, g_done, routed(g, ch - RING))
                    nc.scalar.activation(s_ring[:, ch % RING], up_ps[ch % RING][:], ACT.Silu).then_inc(s_done, 1)

            def hi_part(g, ch):
                if ch == 0:
                    act.wait_ge(s_done, chunks(g, ch))
                else:
                    act.wait_ge(g_done, routed(g, ch))
                need(act, down_done, chunks(g, ch - RING))
                nc.scalar.copy(g_hi[:, ch % RING], g_ring[:, ch % RING]).then_inc(hi_done, 1)

            def step(g, j):
                gu, ch = up_of(g, j)
                silu_part(gu, ch)
                if ch == 0:
                    hi_part(g, NC - 1)
                else:
                    hi_part(gu, ch - 1)

            def finish(g):
                act.wait_ge(down_done, chunks(g, NC - 1))
                modulate(fT, (down_ps, down_ps), GB, None, g).then_inc(f_done, 1)

            act.wait_ge(c_in, 16)
            nc.scalar.activation(cs_sb[:], c_sb[:], ACT.Silu).then_inc(cs_done, 1)
            act.wait_ge(mod_done, 1)
            act.wait_ge(shared_in, 32)
            nc.scalar.copy(up_hi[:, 0, :], shared_raw[:, 0, :]).then_inc(w_hi, 1)
            nc.scalar.copy(down_hi[:, 0, :], shared_raw[:, 1, :]).then_inc(w_hi, 1)

            def split(k):
                act.wait_ge(piece_in[k], 32)
                hi = up_hi if k % 2 == 0 else down_hi
                c0 = 1 + k // 2 * PIECE
                nc.scalar.copy(hi[:, c0:c0 + PIECE, :],
                               stage[:, k % STAGES].rearrange("p (c m) -> p c m", m=P)).then_inc(w_hi, 1)

            norm1(0)
            step_size(0)
            split(0)
            decay(0)
            split(1)
            gate1(0)
            split(2)
            norm2(0)
            split(3)
            router(0)
            split(4)
            act.wait_ge(both_done, 1)
            nc.scalar.copy(sel[:], both[:].unsqueeze(2).broadcast_to([P, E, F])).then_inc(sel_done, 1)
            hand_over(0)
            for k in range(5, 2 * NP):
                split(k)
            silu_part(0, 0)
            for ch in range(1, LAG):
                silu_part(0, ch)
                hi_part(0, ch - 1)
            for j in range(LAG):
                step(0, j)
            with act.Fori(0, G - 1) as g:
                for j in range(LAG, NC):
                    step(g, j)
                    if j == 5:
                        norm1(g + 1)
                    if j == 8:
                        step_size(g + 1)
                    if j == 11:
                        decay(g + 1)
                    if j == 16:
                        gate1(g + 1)
                    if j == 21:
                        norm2(g + 1)
                    if j == 25:
                        router(g + 1)
                    if j == NC - LAG - 1:
                        hand_over(g + 1)
                finish(g)
                for j in range(LAG):
                    step(g + 1, j)
            for j in range(LAG, NC - LAG):
                step(G - 1, j)
            hi_part(G - 1, NC - 1)
            finish(G - 1)

        @block.vector
        def _(dve):
            DVE_LINKS = 85
            chain = {"base": 0, "n": 0}

            def link(ins):
                chain["n"] += 1
                ins.then_inc(dve_own, 1)
                dve.wait_ge(dve_own, chain["base"] + chain["n"])

            def log1p_of(s, s2, p, e_in, dst, plus):
                link(nc.vector.tensor_scalar(p, e_in, 2.0, None, ALU.add))
                link(nc.vector.reciprocal(p, p))
                link(nc.vector.tensor_tensor(s, e_in, p, ALU.mult))
                link(nc.vector.tensor_tensor(s2, s, s, ALU.mult))
                link(nc.vector.tensor_scalar(p, s2, 1.0 / 13, None, ALU.mult))
                for k in (11, 9, 7, 5, 3):
                    link(nc.vector.scalar_tensor_tensor(p, p, 1.0 / k, s2, ALU.add, ALU.mult))
                link(nc.vector.scalar_tensor_tensor(p, p, 1.0, s, ALU.add, ALU.mult))
                link(nc.vector.scalar_tensor_tensor(dst, p, 2.0, plus, ALU.mult, ALU.add))

            def statistics(g):
                for t in range(TL):
                    last = nc.vector.bn_stats(stats[:, t], x_sb[:, g, t])
                link(last)
                nc.vector.memset(pad[:], 0.0)
                for t in range(TL):
                    last = nc.vector.bn_aggr(mv[:, t], stats[:, t])
                link(last)
                v, y, a = rs[:, 0], rs[:, 1], rs[:, 2]
                link(nc.vector.tensor_scalar(v, mv[:, :, 1], LN_EPS, None, ALU.add))
                link(nc.vector.tensor_scalar(y.bitcast(i32), v.bitcast(i32), -0.5, RSQRT_GUESS, ALU.mult, ALU.add))
                for _ in range(RSQRT_STEPS):
                    link(nc.vector.tensor_tensor(a, y, y, ALU.mult))
                    link(nc.vector.scalar_tensor_tensor(a, a, -0.5, v, ALU.mult, ALU.mult))
                    link(nc.vector.scalar_tensor_tensor(y, a, 1.5, y, ALU.add, ALU.mult))

            def normalise(g):
                for t in range(TL):
                    last = nc.vector.tensor_scalar(xn[:, t], x_sb[:, g, t], mv[:, t, 0:1], rs[:, 1, t:t + 1],
                                                   ALU.subtract, ALU.mult)
                return last

            def step_size_in(g):
                dve.wait_ge(b_ps, g + 1)
                link(nc.vector.tensor_scalar(sp[:, 0], T_ps[:, 0:TL], bd_sb[:, 0:1], None, ALU.add))
                link(nc.vector.scalar_tensor_tensor(sp[:, 1], sp[:, 0], -1.0, sp[:, 0], ALU.mult, ALU.max))
                nc.vector.tensor_scalar(sp[:, 1], sp[:, 1], 1.0, None, ALU.add).then_inc(spz_done, 1)
                link(nc.vector.tensor_scalar(sp[:, 3], sp[:, 0], 0.0, None, ALU.max))

            def step_size(g):
                dve.wait_ge(sps_done, g + 1)
                dve.wait_ge(spz_done, g + 1)
                link(nc.vector.tensor_tensor(sp[:, 4], sp[:, 1], sp[:, 2], ALU.add))
                link(nc.vector.reciprocal(sp[:, 4], sp[:, 4]))
                link(nc.vector.scalar_tensor_tensor(sp[:, 5], sp[:, 2], -EULER, sp[:, 4], ALU.mult, ALU.mult))
                log1p_of(sp[:, 6], sp[:, 7], sp[:, 4], sp[:, 5], sp[:, 0], sp[:, 3])
                nc.vector.tensor_copy(delta_b[:], sp[:, 0].unsqueeze(2).broadcast_to([P, TL, N])).then_inc(delta_done, 1)

            def decay_in(g):
                dve.wait_ge(delta_ps, g + 1)
                nc.vector.tensor_scalar(uc_sb[:], Q_ps[:, S:2 * S], A_sb[:, 0:1], U_POLY, ALU.mult,
                                        ALU.min).then_inc(uc_done, 1)
                link(nc.vector.tensor_scalar(u_sb[:], Q_ps[:, S:2 * S], A_sb[:, 0:1], None, ALU.mult))
                link(nc.vector.tensor_scalar(p_sb[:], u_sb[:], 1.0 / 120, 1.0 / 24, ALU.mult, ALU.add))
                nc.vector.tensor_scalar(mask_u[:], u_sb[:], U_POLY, None, ALU.is_gt)
                link(nc.vector.tensor_tensor(p_sb[:], p_sb[:], u_sb[:], ALU.mult))
                link(nc.vector.scalar_tensor_tensor(p_sb[:], p_sb[:], 1.0 / 6, u_sb[:], ALU.add, ALU.mult))

            def decay_poly(g):
                link(nc.vector.scalar_tensor_tensor(p_sb[:], p_sb[:], 0.5, u_sb[:], ALU.add, ALU.mult))
                link(nc.vector.scalar_tensor_tensor(p_sb[:], p_sb[:], 1.0, u_sb[:], ALU.add, ALU.mult))
                link(nc.vector.tensor_scalar(p_sb[:], p_sb[:], 1.0, None, ALU.add))

            def decay(g):
                dve.wait_ge(su_done, g + 1)
                dve.wait_ge(uc_done, g + 1)
                link(nc.vector.tensor_tensor(dB[:], uc_sb[:], su_sb[:], ALU.subtract))
                link(nc.vector.reciprocal(dB[:], dB[:]))
                link(nc.vector.tensor_tensor(dA[:], su_sb[:], dB[:], ALU.mult))
                nc.vector.memset(Ct[:, 0:1], 1.0)
                link(nc.vector.copy_predicated(dA[:], mask_u[:], p_sb[:]))

            def state_in(g):
                nc.vector.tensor_tensor_scan(Ct[:, 1:S], dA[:, 0:S - 1], zeros[:, 0:S - 1], 1.0, ALU.mult, ALU.add)
                link(nc.vector.tensor_scalar(p_sb[:], dA[:], -1.0, rA[:, 0:1], ALU.add, ALU.mult))
                link(nc.vector.scalar_tensor_tensor(dB[:], Q_ps[:, 0:S], bB_sb[:, 0:1], p_sb[:], ALU.add, ALU.mult))

            def state_sum(g):
                link(nc.vector.tensor_scalar(u_sb[:], Ct[:], SSM_EPS, None, ALU.add))
                link(nc.vector.reciprocal(u_sb[:], u_sb[:]))
                link(nc.vector.tensor_tensor(dB[:], dB[:], u_sb[:], ALU.mult))
                link(nc.vector.tensor_tensor_scan(p_sb[:], dB[:], zeros[:], 0.0, ALU.add, ALU.add))

            def state_out(g):
                link(nc.vector.tensor_tensor(p_sb[:], p_sb[:], Ct[:], ALU.mult))
                nc.vector.tensor_tensor(y_sb[:], p_sb[:], Ct[:], ALU.mult).then_inc(y_done, 1)

            def residual1(g):
                dve.wait_ge(u_ps, g + 1)
                link(nc.vector.tensor_tensor(x_sb[:, g].rearrange("p t d -> p (t d)"),
                                             x_sb[:, g].rearrange("p t d -> p (t d)"), Q_ps[:], ALU.add))

            def router_in(g):
                dve.wait_ge(aff_ps, g + 1)
                q = Q_ps[:, 0:TL * E].rearrange("p (t e) -> p t e", e=E)
                link(nc.vector.tensor_copy(aff[:], q))
                nc.vector.scalar_tensor_tensor(az[:], aff[:], -1.0, aff[:], ALU.mult, ALU.max).then_inc(az_done, 1)
                link(nc.vector.tensor_tensor(biased[:], q, bias_sb[:].unsqueeze(1).broadcast_to([P, TL, E]), ALU.add))

            def router_top(g):
                for t in range(TL):
                    last = nc.vector.max(top[:, t], biased[:, t])
                link(last)
                nc.vector.memset(pad[:], 0.0)
                for t in range(TL):
                    last = nc.vector.match_replace(left[:, t], top[:, t], biased[:, t], LOWEST)
                link(last)
                link(nc.vector.tensor_tensor(chosen[:], left[:], biased[:], ALU.not_equal))

            def router_sigmoid(g):
                dve.wait_ge(sz_done, g + 1)
                dve.wait_ge(az_done, g + 1)
                link(nc.vector.scalar_tensor_tensor(az[:], az[:], 1.0, sz[:], ALU.add, ALU.add))
                link(nc.vector.scalar_tensor_tensor(aff[:], aff[:], 0.0, az[:], ALU.is_ge, ALU.mult))
                nc.vector.scalar_tensor_tensor(aff[:], sz[:], -EULER, aff[:], ALU.mult, ALU.max)
                link(nc.vector.scalar_tensor_tensor(az[:], sz[:], -EULER, az[:], ALU.mult, ALU.add))
                link(nc.vector.reciprocal(az[:], az[:]))
                link(nc.vector.tensor_tensor(ez[:], aff[:], az[:], ALU.mult))

            def router_out(g):
                link(nc.vector.tensor_tensor(ez[:], ez[:], chosen[:], ALU.mult))
                link(nc.vector.tensor_reduce(wsum[:], ez[:], AX.X, ALU.add))
                link(nc.vector.tensor_scalar(wsum[:], wsum[:], SUM_EPS, None, ALU.add))
                link(nc.vector.reciprocal(wsum[:], wsum[:]))
                link(nc.vector.tensor_tensor(ez[:], ez[:], wsum[:].unsqueeze(2).broadcast_to([P, TL, E]), ALU.mult))
                link(nc.vector.tensor_copy(cw_hl[:, :, 0], ez[:]))
                nc.vector.tensor_tensor(cw_hl[:, :, 1], ez[:], cw_hl[:, :, 0].bitcast(fp32),
                                        ALU.subtract).then_inc(cw_done, 1)

            def hand_over(g):
                dve.wait_ge(h2hi_done, g + 1)
                nc.vector.tensor_tensor(h2_lo[:], h2T[:], h2_hi[:].bitcast(fp32), ALU.subtract).then_inc(h2lo_done, 1)

            def weigh(g, ch):
                if ch == 0:
                    return
                dve.wait_ge(s_done, chunks(g, ch))
                dve.wait_ge(bc_done, routed(g, ch))
                need(dve, lo_done, chunks(g, ch - RING))
                nc.vector.tensor_tensor(g_ring[:, ch % RING], s_ring[:, ch % RING], cw_ps[ch % 2][:],
                                        ALU.mult).then_inc(g_done, 1)

            def finish(g):
                dve.wait_ge(f_ps, g + 1)
                need(dve, out_done, 16 * g)
                nc.vector.tensor_tensor(out_sb[:].rearrange("p t d -> p (t d)"),
                                        x_sb[:, g].rearrange("p t d -> p (t d)"), Q_ps[:], ALU.add).then_inc(out_ready, 1)

            dve.wait_ge(vec_in, 16 * 8)
            W = lambda i: wk[:, i:i + 1]
            LN2_HI, LN2_LO, MAGIC = 0.693359375, -2.12194440e-4, 12582912.0
            link(nc.vector.scalar_tensor_tensor(W(1), W(0), -1.0, W(0), ALU.mult, ALU.max))
            link(nc.vector.tensor_scalar(W(1), W(1), 80.0, None, ALU.min))
            link(nc.vector.tensor_scalar(W(2), W(1), 1.4426950408889634, MAGIC, ALU.mult, ALU.add))
            link(nc.vector.tensor_scalar(W(2), W(2), -MAGIC, None, ALU.add))
            link(nc.vector.scalar_tensor_tensor(W(3), W(2), -LN2_HI, W(1), ALU.mult, ALU.add))
            link(nc.vector.scalar_tensor_tensor(W(3), W(2), -LN2_LO, W(3), ALU.mult, ALU.add))
            link(nc.vector.tensor_scalar(W(3), W(3), -1.0, None, ALU.mult))
            link(nc.vector.tensor_scalar(W(4), W(3), 1.0 / 5040, 1.0 / 720, ALU.mult, ALU.add))
            link(nc.vector.tensor_tensor(W(4), W(4), W(3), ALU.mult))
            for f in (120.0, 24.0, 6.0, 2.0, 1.0):
                link(nc.vector.scalar_tensor_tensor(W(4), W(4), 1.0 / f, W(3), ALU.add, ALU.mult))
            link(nc.vector.tensor_scalar(wki[:], W(2), -8388608.0, 127.0 * 8388608.0, ALU.mult, ALU.add))
            link(nc.vector.scalar_tensor_tensor(W(5), W(4), 1.0, wki[:].bitcast(fp32), ALU.add, ALU.mult))
            link(nc.vector.tensor_scalar(W(6), W(0), 0.0, None, ALU.max))
            log1p_of(W(7), W(8), W(9), W(5), W(10), W(6))
            link(nc.vector.tensor_scalar(A_sb[:], W(10), -1.0, None, ALU.mult))
            link(nc.vector.tensor_scalar(rA[:], A_sb[:], SSM_EPS, None, ALU.add))
            link(nc.vector.reciprocal(rA[:], rA[:]))
            dve.wait_ge(x_in[0], 16)
            statistics(0)
            dve.wait_ge(csT_ps, 1)
            nc.vector.tensor_copy(cs_T[:], Q_ps[:, 0:BATCH]).then_inc(csT_done, 1)
            normalise(0).then_inc(xn1_done, 1)
            dve.wait_ge(wT_ps, 1)
            nc.vector.tensor_copy(WB_T[:], T_ps[:, 128:128 + N])
            nc.vector.tensor_copy(Wo_T[:], T_ps[:, 256:256 + D])
            nc.vector.tensor_copy(cent_T[:], T_ps[:, 384:384 + E]).then_inc(wT_done, 1)
            dve.wait_ge(mod_ps, 1)
            m = Q_ps[:, 0:6 * BATCH].rearrange("p (r b) -> p r b", b=BATCH)
            link(nc.vector.tensor_copy(mod[:, 0:6], m))
            for r in (CA, CB):
                nc.vector.tensor_scalar(mod[:, r], mod[:, r], 1.0, None, ALU.add)
            for i, r in enumerate((GA, GB)):
                last = nc.vector.tensor_scalar(sgn[:, i], mod[:, r], 0.0, 2.0, ALU.is_ge, ALU.mult)
            link(last)
            for i, r in enumerate((GA, GB)):
                last = nc.vector.tensor_scalar(sgn[:, i], sgn[:, i], -1.0, None, ALU.add)
            link(last)
            for i, r in enumerate((GA, GB)):
                last = nc.vector.scalar_tensor_tensor(mod[:, r], mod[:, r], -1.0, mod[:, r], ALU.mult, ALU.max)
            link(last)
            for i, r in enumerate((GA, GB)):
                last = nc.vector.scalar_tensor_tensor(mod[:, r], mod[:, r], 0.25, sgn[:, i], ALU.max, ALU.mult)
            link(last)
            nc.vector.tensor_scalar(mod[:, BOGA], mod[:, GA], bo_sb[:, 0:1], None, ALU.mult).then_inc(mod_done, 1)
            dve.wait_ge(ident_done, 2)
            nc.vector.tensor_tensor(both[:], ident[:, 0:E], ident[:, E:2 * E], ALU.add).then_inc(both_done, 1)
            step_size_in(0)
            step_size(0)
            decay_in(0)
            decay_poly(0)
            decay(0)
            state_in(0)
            state_sum(0)
            state_out(0)
            residual1(0)
            statistics(0)
            normalise(0).then_inc(xn2_done, 1)
            router_in(0)
            router_top(0)
            router_sigmoid(0)
            router_out(0)
            hand_over(0)
            for ch in range(LAG):
                weigh(0, ch)
            for j in range(LAG):
                weigh(*up_of(0, j))
            for k in range(1, G):
                dve.wait_ge(x_in[k], 16)
            setup_links = chain["n"]
            with dve.Fori(0, G - 1) as g:
                chain["base"], chain["n"] = g * DVE_LINKS + setup_links, 0
                for j in range(LAG, NC):
                    weigh(*up_of(g, j))
                    if j == 3:
                        statistics(g + 1)
                    if j == 4:
                        normalise(g + 1).then_inc(xn1_done, 1)
                    if j == 7:
                        step_size_in(g + 1)
                    if j == 8:
                        step_size(g + 1)
                    if j == 10:
                        decay_in(g + 1)
                    if j == 11:
                        decay_poly(g + 1)
                    if j == 12:
                        decay(g + 1)
                    if j == 13:
                        state_in(g + 1)
                    if j == 14:
                        state_sum(g + 1)
                    if j == 15:
                        state_out(g + 1)
                    if j == 18:
                        residual1(g + 1)
                    if j == 19:
                        statistics(g + 1)
                    if j == 20:
                        normalise(g + 1).then_inc(xn2_done, 1)
                    if j == 23:
                        router_in(g + 1)
                    if j == 24:
                        router_top(g + 1)
                    if j == 26:
                        router_sigmoid(g + 1)
                    if j == 27:
                        router_out(g + 1)
                    if j == NC - LAG - 1:
                        hand_over(g + 1)
                for j in range(LAG):
                    weigh(*up_of(g + 1, j))
                    if j == 2:
                        finish(g)
                assert chain["n"] == DVE_LINKS, chain["n"]
            for j in range(LAG, NC - LAG):
                weigh(*up_of(G - 1, j))
            finish(G - 1)

        @block.tensor
        def _(pe):
            def transpose_tiles(dst, src):
                for t in range(TL):
                    last = nc.tensor.transpose(dst[:, t * P:(t + 1) * P], src(t), ident[:])
                return last

            def norm1(g):
                pe.wait_ge(xn1_done, g + 1)
                transpose_tiles(T_ps, lambda t: xn[:, t]).then_inc(xn1_ps, 1)

            def project(g):
                pe.wait_ge(h1_done, g + 1)
                for half in range(2):
                    nc.tensor.matmul(Q_ps[half * N:(half + 1) * N, 0:S], WB_T[:], h1T[:, half * S:(half + 1) * S],
                                     start=True, stop=True)
                for t in range(TL):
                    last = nc.tensor.matmul(T_ps[:, t:t + 1], h1T[:, t * P:(t + 1) * P], Wd_sb[:], start=True, stop=True)
                last.then_inc(b_ps, 1)

            def spread(g):
                pe.wait_ge(delta_done, g + 1)
                for t in range(TL):
                    half, col = t // (TL // 2), S + t % (TL // 2) * P
                    last = nc.tensor.matmul(Q_ps[half * N:(half + 1) * N, col:col + P], delta_b[:, t], ident[:],
                                            start=True, stop=True)
                last.then_inc(delta_ps, 1)

            def state_out(g):
                pe.wait_ge(y_done, g + 1)
                for half in range(2):
                    rows = slice(half * N, (half + 1) * N)
                    last = nc.tensor.matmul((T_ps, Q_ps)[half][:, half * S:(half + 1) * S], Wo_T[rows, :], y_sb[rows, :],
                                            start=True, stop=True)
                last.then_inc(y_ps, 1)

            def residual1(g):
                pe.wait_ge(u_done, g + 1)
                transpose_tiles(Q_ps, lambda t: uT[:, t * P:(t + 1) * P]).then_inc(u_ps, 1)

            def norm2(g):
                pe.wait_ge(xn2_done, g + 1)
                transpose_tiles(T_ps, lambda t: xn[:, t]).then_inc(xn2_ps, 1)

            def affinities(g):
                pe.wait_ge(h2_done, g + 1)
                for t in range(TL):
                    last = nc.tensor.matmul(Q_ps[:, t * E:(t + 1) * E], h2T[:, t * P:(t + 1) * P], cent_T[:],
                                            start=True, stop=True)
                last.then_inc(aff_ps, 1)

            def route(g):
                pe.wait_ge(cw_done, g + 1)
                transpose_tiles(T_ps, lambda t: cw_hl[:, t].rearrange("p h e -> p (h e)").bitcast(fp32)).then_inc(cwT_ps, 1)

            def up(g, ch):
                if ch == 0:
                    pe.wait_ge(h2hi_done, g + 1)
                    need(pe, s_done, chunks(g - 1, NC - RING))
                else:
                    need(pe, s_done, chunks(g, ch - RING))
                u = up_ps[ch % RING]
                nc.tensor.matmul(u[:], up_lo[:, ch, :], h2_hi[:], start=True, stop=False)
                if ch == 0:
                    nc.tensor.matmul(u[:], up_hi[:, ch, :], h2_hi[:], start=False, stop=False)
                    pe.wait_ge(h2lo_done, g + 1)
                    nc.tensor.matmul(u[:], up_hi[:, ch, :], h2_lo[:], start=False, stop=True).then_inc(up_done, 1)
                    return
                nc.tensor.matmul(u[:], up_hi[:, ch, :], h2_hi[:], start=False, stop=False)
                nc.tensor.matmul(u[:], up_hi[:, ch, :], h2_lo[:], start=False, stop=True).then_inc(up_done, 1)
                if ch == 1:
                    pe.wait_ge(cwT_done, g + 1)
                need(pe, g_done, routed(g, ch - 2))
                nc.tensor.matmul(cw_ps[ch % 2][:], sel[:, 2 * ch - 2:2 * ch, :].rearrange("p e f -> p (e f)"), cw_T[:],
                                 start=True, stop=True).then_inc(bc_done, 1)

            def down(g, ch):
                if ch == 0:
                    need(pe, f_done, g)
                pe.wait_ge(hi_done, chunks(g, ch))
                nc.tensor.matmul(down_ps[:], down_lo[:, ch, :], g_hi[:, ch % RING], start=ch == 0, stop=False)
                nc.tensor.matmul(down_ps[:], down_hi[:, ch, :], g_hi[:, ch % RING], start=False, stop=False)
                pe.wait_ge(lo_done, chunks(g, ch))
                nc.tensor.matmul(down_ps[:], down_hi[:, ch, :], g_lo[:, ch % RING], start=False,
                                 stop=ch == NC - 1).then_inc(down_done, 1)

            def finish(g):
                pe.wait_ge(f_done, g + 1)
                transpose_tiles(Q_ps, lambda t: fT[:, t * P:(t + 1) * P]).then_inc(f_ps, 1)

            pe.wait_ge(ident_done, 1)
            pe.wait_ge(cs_done, 1)
            nc.tensor.transpose(Q_ps[:, 0:BATCH], cs_sb[:], ident[0:BATCH, 0:BATCH]).then_inc(csT_ps, 1)
            pe.wait_ge(WB_in, 16)
            nc.tensor.transpose(T_ps[:, 128:128 + N], WB_sb[:], ident[0:N, 0:N])
            pe.wait_ge(Wo_in, 32)
            nc.tensor.transpose(T_ps[:, 256:256 + D], Wo_sb[:].rearrange("d h n -> d (h n)"), ident[:])
            pe.wait_ge(cent_in, 16)
            nc.tensor.transpose(T_ps[:, 384:384 + E], cent_sb[:], ident[0:E, 0:E]).then_inc(wT_ps, 1)
            pe.wait_ge(csT_done, 1)
            pe.wait_ge(wmod_in, 16)
            for r in range(6):
                last = nc.tensor.matmul(Q_ps[:, r * BATCH:(r + 1) * BATCH], wmod_sb[:, r * D:(r + 1) * D], cs_T[:],
                                        start=True, stop=True)
            last.then_inc(mod_ps, 1)
            pe.wait_ge(wT_done, 1)
            norm1(0)
            pe.wait_ge(mod_done, 1)
            project(0)
            spread(0)
            state_out(0)
            residual1(0)
            norm2(0)
            affinities(0)
            route(0)
            pe.wait_ge(w_lo, 2 * NP + 1)
            pe.wait_ge(sel_done, 1)
            for ch in range(LAG):
                up(0, ch)
            for j in range(LAG):
                up(*up_of(0, j))
                down(0, j)
            with pe.Fori(0, G - 1) as g:
                for j in range(LAG, NC):
                    up(*up_of(g, j))
                    if j == 5:
                        norm1(g + 1)
                    if j == 7:
                        project(g + 1)
                    if j == 10:
                        spread(g + 1)
                    if j == 16:
                        state_out(g + 1)
                    if j == 18:
                        residual1(g + 1)
                    if j == 21:
                        norm2(g + 1)
                    if j == 23:
                        affinities(g + 1)
                    if j == 28:
                        route(g + 1)
                    down(g, j)
                for j in range(LAG):
                    up(*up_of(g + 1, j))
                    if j == 1:
                        finish(g)
                    down(g + 1, j)
            for j in range(LAG, NC - LAG):
                up(*up_of(G - 1, j))
                down(G - 1, j)
            for ch in range(NC - LAG, NC):
                down(G - 1, ch)
            finish(G - 1)


_INS = ["L0_attn_x", "L0_attn_A_log", "L0_attn_WB", "L0_attn_bB", "L0_attn_Wd", "L0_attn_bd", "L0_attn_Wo",
        "L0_attn_bo", "L0_ffn_centroids", "L0_ffn_expert_biases", "L0_ffn_Ws_up", "L0_ffn_Ws_down",
        "L0_ffn_W_up", "L0_ffn_W_down", "L0_c", "L0_wmod"]


def kernel(**inputs):
    import numpy as _np
    import concourse.bacc as _bacc
    from concourse import mybir as _mybir
    from concourse.bass_utils import run_bass_kernel_spmd as _run

    nc = _bacc.Bacc("TRN2", target_bir_lowering=False, num_devices=1)
    arrays, args = {}, []
    for name in _INS:
        a = _np.ascontiguousarray(inputs[name])
        arrays[f"in_{name}"] = a
        args.append(nc.dram_tensor(f"in_{name}", a.shape, _mybir.dt.from_np(a.dtype), kind="ExternalInput").ap())
    shape = inputs["L0_attn_x"].shape
    args.append(nc.dram_tensor("out_0", shape, _mybir.dt.float32, kind="ExternalOutput").ap())
    adaln_ssm_moe_kernel(nc, *args)
    r = _run(nc, [arrays], core_ids=[0])
    return r.results[0]["out_0"]
```

```python
import concourse.bass as bass
from concourse import mybir
from contextlib import ExitStack


def adaln_ssm_moe_kernel(nc, x, A_log, WB, bB, Wd, bd, Wo, bo, centroids, expert_biases,
                         Ws_up, Ws_down, W_up, W_down, c, wmod, out):
    fp32 = mybir.dt.float32
    r32 = mybir.dt.float32r
    i32 = mybir.dt.int32
    ALU = mybir.AluOpType
    ACT = mybir.ActivationFunctionType
    AX = mybir.AxisListType

    P = 128
    BATCH, S, D = x.shape
    N = A_log.shape[0]
    E, _, F = W_up.shape
    GT = 2 * S
    G = BATCH * S // GT
    TL = GT // P
    NC = E * F // P + 1
    NR = NC - 1
    RING = 3
    LAG = 4
    TURN = 3
    TOPK = 8
    LN_EPS, SSM_EPS, SUM_EPS = 1e-5, 1e-6, 1e-8
    EXP_C = (0.5000000095, 0.1666651860, 0.0416662051, 0.0083689186, 0.0013950541)
    LOG2E, LN2, MAGIC = 1.4426950408889634, 0.6931471805599453, 12582912.0
    MANT, U_LEAST = 8388608.0, -87.0
    ATANH_D = (0.3333320657, 0.2001084955, 0.1399957025, 0.1401223059)
    LOWEST = -3.0e38
    EULER = 2.718281828459045
    RSQRT_GUESS, RSQRT_STEPS = float(0x5F3759DF), 3
    SA, CA, GA, SB, CB, GB, BOGA = range(7)
    PIECE = 8
    NP = NR // PIECE
    STAGES = 4
    assert D == P and 2 * N == P and 2 * F == P and NC % RING == 0 and NR % 2 == 0 and NR % PIECE == 0

    x_v = x.rearrange("b s d -> (b s) d").rearrange("(g t p) d -> g p t d", t=TL, p=P)
    out_v = out.rearrange("b s d -> (b s) d").rearrange("(g t p) d -> g p t d", t=TL, p=P)
    up_v = W_up.rearrange("e d f -> d e f")
    down_v = W_down.rearrange("e f d -> (e f) d").rearrange("(c p) d -> p c d", p=P)

    ctx = ExitStack()
    with ctx:
        def sb(name, shape, dt=fp32):
            return ctx.enter_context(nc.sbuf_tensor(name, shape, dt))

        def sem(name):
            return ctx.enter_context(nc.semaphore(name))

        x_sb = sb("x_sb", [P, G, TL, D])
        ident = sb("ident", [P, P])
        both = sb("both", [P, E])
        sel = sb("sel", [P, E, F], r32)
        stage = sb("stage", [P, STAGES, PIECE * P])
        shared_raw = sb("shared_raw", [P, 2, P])
        up_hi = sb("up_hi", [P, NC, P], r32)
        up_lo = sb("up_lo", [P, NC, P], r32)
        down_hi = sb("down_hi", [P, NC, P], r32)
        down_lo = sb("down_lo", [P, NC, P], r32)
        WB_sb = sb("WB_sb", [N, D])
        Wd_sb = sb("Wd_sb", [D, 1])
        Wo_sb = sb("Wo_sb", [P, 2, N])
        cent_sb = sb("cent_sb", [E, D])
        WB_T = sb("WB_T", [D, N])
        Wo_T = sb("Wo_T", [P, D])
        cent_T = sb("cent_T", [D, E])
        bB_sb = sb("bB_sb", [P, 1])
        bd_sb = sb("bd_sb", [P, 1])
        bo_sb = sb("bo_sb", [D, 1])
        bias_sb = sb("bias_sb", [P, E])
        A_sb = sb("A_sb", [P, 1])
        rA = sb("rA", [P, 1])
        pad = sb("pad", [P, 1])
        act_pad = sb("act_pad", [P, 1])
        minus_one = sb("minus_one", [P, 1])
        wk = sb("wk", [P, 16])
        wki = sb("wki", [P, 1], i32)
        c_sb = sb("c_sb", [BATCH, D])
        cs_sb = sb("cs_sb", [BATCH, D])
        cs_T = sb("cs_T", [D, BATCH])
        wmod_sb = sb("wmod_sb", [D, 6 * D])
        mod = sb("mod", [D, 7, BATCH])
        sgn = sb("sgn", [D, 2, BATCH])
        stats = sb("stats", [P, TL, 6])
        mv = sb("mv", [P, TL, 2])
        rs = sb("rs", [P, 2, TL])
        ln2 = sb("ln2", [P, 2, TL])
        mv1 = sb("mv1", [P, G, TL, 2])
        rs1 = sb("rs1", [P, 2, G, TL])
        ln1 = sb("ln1", [P, 2, G, TL])
        xn1 = sb("xn1", [P, TL, D])
        xn2 = sb("xn2", [P, TL, D])
        h1T = sb("h1T", [D, GT])
        sp = sb("sp", [P, 8, TL])
        delta_b = sb("delta_b", [P, TL, N])
        u_sb = sb("u_sb", [P, S])
        n_sb = sb("n_sb", [P, S])
        p_sb = sb("p_sb", [P, S])
        pow2 = sb("pow2", [P, S], i32)
        dA = sb("dA", [P, S])
        Ct = sb("Ct", [P, S])
        dB = sb("dB", [P, S])
        zeros = sb("zeros", [P, S])
        s_sum = sb("s_sum", [P, S])
        y_sb = sb("y_sb", [P, S])
        uT = sb("uT", [D, GT])
        h2T = sb("h2T", [D, GT])
        aff = sb("aff", [P, TL, E])
        biased = sb("biased", [P, TL, E])
        left = sb("left", [P, TL, E])
        top = sb("top", [P, TL, TOPK])
        az = sb("az", [P, TL, E])
        sz = sb("sz", [P, TL, E])
        ez = sb("ez", [P, TL, E])
        wsum = sb("wsum", [P, TL])
        cw_hl = sb("cw_hl", [P, TL, 2, E], r32)
        h2_hi = sb("h2_hi", [D, GT], r32)
        h2_lo = sb("h2_lo", [D, GT], r32)
        cw_T = sb("cw_T", [2 * E, GT], r32)
        s_ring = sb("s_ring", [P, RING, GT])
        g_ring = sb("g_ring", [P, RING, GT])
        g_hi = sb("g_hi", [P, RING, GT], r32)
        g_lo = sb("g_lo", [P, RING, GT], r32)
        fT = sb("fT", [D, GT])
        out_sb = sb("out_sb", [P, TL, D])

        def bank(name):
            return ctx.enter_context(nc.psum_tensor(name, [P, GT], fp32))

        up_ps = [bank(f"up_ps{i}") for i in range(RING)]
        cw_ps = [bank(f"cw_ps{i}") for i in range(2)]
        down_ps = bank("down_ps")
        T_ps = bank("T_ps")
        Q_ps = bank("Q_ps")

        x_in = [sem(f"x_in{i}") for i in range(G)]
        c_in, wmod_in, vec_in, WB_in, Wo_in, cent_in = (sem(n) for n in (
            "c_in", "wmod_in", "vec_in", "WB_in", "Wo_in", "cent_in"))
        shared_in = sem("shared_in")
        piece_in = [sem(f"piece_in{i}") for i in range(2 * NP)]
        out_done = sem("out_done")
        ident_done, pool_own, act_own, dve_own = (sem(n) for n in ("ident_done", "pool_own", "act_own", "dve_own"))
        shared_clear, both_done, sel_done = (sem(n) for n in ("shared_clear", "both_done", "sel_done"))
        cs_done, csT_ps, csT_done, mod_ps, mod_done = (sem(n) for n in (
            "cs_done", "csT_ps", "csT_done", "mod_ps", "mod_done"))
        wT_ps, wT_done = sem("wT_ps"), sem("wT_done")
        rs_first, ln1_done = sem("rs_first"), sem("ln1_done")
        w_hi, w_lo = sem("w_hi"), sem("w_lo")
        names = ("xn1_done", "xn1_ps", "h1_done", "d_ps", "b_ps", "z_done", "sps_done", "delta_done", "delta_ps",
                 "sum_done", "ss_done", "y_done", "ln2_done", "y_ps", "u_done", "u_ps", "xn2_done", "xn2_ps", "h2_done",
                 "aff_ps", "aff_done", "az_done", "sz_done", "cw_done", "cwT_ps", "h2hi_done", "h2lo_done", "cwT_done",
                 "f_done", "f_ps", "out_ready")
        (xn1_done, xn1_ps, h1_done, d_ps, b_ps, z_done, sps_done, delta_done, delta_ps,
         sum_done, ss_done, y_done, ln2_done, y_ps, u_done, u_ps, xn2_done, xn2_ps, h2_done,
         aff_ps, aff_done, az_done, sz_done, cw_done, cwT_ps, h2hi_done, h2lo_done, cwT_done,
         f_done, f_ps, out_ready) = (sem(n) for n in names)
        up_done, bc_done, s_done, g_done, hi_done, lo_done, down_done = (sem(n) for n in (
            "up_done", "bc_done", "s_done", "g_done", "hi_done", "lo_done", "down_done"))

        def need(eng, s, value):
            if not isinstance(value, int) or value > 0:
                eng.wait_ge(s, value)

        def chunks(g, ch):
            return g * NC + (ch + 1)

        def routed(g, ch):
            return g * NR + ch

        UP, WEIGH, PARTS = LAG, LAG - 1, LAG - 2

        def at(g, i):
            return (g, i) if i < NC else (g + 1, i - NC)

        block = ctx.enter_context(nc.Block())

        @block.sync
        def _(sync):
            sync.sem_inc(out_done, 16)
            sync.dma_start(c_sb[:], c).then_inc(c_in, 16)
            sync.dma_start(x_sb[:, 0], x_v[0]).then_inc(x_in[0], 16)
            sync.dma_start(wmod_sb[:], wmod).then_inc(wmod_in, 16)
            sync.dma_start(WB_sb[:], WB).then_inc(WB_in, 16)
            for h in range(2):
                sync.dma_start(wk[h * N:(h + 1) * N, 0:1], A_log.rearrange("(n o) -> n o", o=1)).then_inc(vec_in, 16)
                sync.dma_start(bB_sb[h * N:(h + 1) * N, :], bB.rearrange("(n o) -> n o", o=1)).then_inc(vec_in, 16)
                sync.dma_start(Wo_sb[:, h, :], Wo).then_inc(Wo_in, 16)
            sync.dma_start(Wd_sb[:], Wd.rearrange("o d -> d o")).then_inc(vec_in, 16)
            sync.dma_start(bo_sb[:], bo.rearrange("(d o) -> d o", o=1)).then_inc(vec_in, 16)
            sync.dma_start(bd_sb[:], bd.rearrange("(o n) -> o n", o=1).broadcast_to([P, 1])).then_inc(vec_in, 16)
            sync.dma_start(bias_sb[:], expert_biases.rearrange("(o n) -> o n", o=1).broadcast_to([P, E])).then_inc(vec_in, 16)
            sync.dma_start(cent_sb[:], centroids).then_inc(cent_in, 16)
            sync.wait_ge(shared_clear, 1)
            sync.dma_start(shared_raw[:, 0, 0:F], Ws_up).then_inc(shared_in, 16)
            sync.dma_start(shared_raw[0:F, 1, :], Ws_down).then_inc(shared_in, 16)
            for k in range(2 * NP):
                i = k // 2
                if k >= STAGES:
                    sync.wait_ge(w_lo, k - STAGES + 2)
                if k % 2 == 0:
                    for e0 in range(0, 2 * PIECE, PIECE):
                        sync.dma_start(
                            stage[:, k % STAGES, e0 * F:(e0 + PIECE) * F].rearrange("d (e f) -> d e f", f=F),
                            up_v[:, i * 2 * PIECE + e0:i * 2 * PIECE + e0 + PIECE, :]).then_inc(piece_in[k], 16)
                else:
                    for c0 in range(0, PIECE, PIECE // 2):
                        sync.dma_start(
                            stage[:, k % STAGES, c0 * P:(c0 + PIECE // 2) * P].rearrange("p (c d) -> p c d", d=D),
                            down_v[:, i * PIECE + c0:i * PIECE + c0 + PIECE // 2, :]).then_inc(piece_in[k], 16)
                if k >= 1 and k < G:
                    sync.dma_start(x_sb[:, k], x_v[k]).then_inc(x_in[k], 16)
            with sync.Fori(0, G) as g:
                sync.wait_ge(out_ready, g + 2)
                sync.dma_start(out_v[bass.ds(g, 1)].rearrange("o p t d -> (o p) t d"), out_sb[:]).then_inc(out_done, 16)
            sync.wait_ge(out_done, 16 * (G + 1))

        @block.gpsimd
        def _(pool):
            nc.gpsimd.memset(shared_raw[:], 0.0).then_inc(shared_clear, 1)
            nc.gpsimd.memset(ident[:], 0.0).then_inc(pool_own, 1)
            pool.wait_ge(pool_own, 1)
            nc.gpsimd.affine_select(out=ident[:], in_=ident[:], compare_op=ALU.not_equal, fill=1.0, base=0,
                                    pattern=[[-1, P]], channel_multiplier=1).then_inc(ident_done, 1)
            nc.gpsimd.memset(minus_one[:], -1.0).then_inc(ident_done, 1)
            nc.gpsimd.memset(zeros[:], 0.0).then_inc(ident_done, 1)

            def state_out(g):
                pool.wait_ge(sum_done, g + 1)
                nc.gpsimd.tensor_tensor(s_sum[:], s_sum[:], Ct[:], ALU.mult).then_inc(ss_done, 1)
                pool.wait_ge(ss_done, g + 1)
                nc.gpsimd.tensor_tensor(y_sb[:], s_sum[:], Ct[:], ALU.mult).then_inc(y_done, 1)

            for k in range(2 * NP + 1):
                pool.wait_ge(w_hi, 2 * (k + 1) if k == 0 else k + 2)
                if k == 0:
                    nc.gpsimd.tensor_tensor(up_lo[:, 0, :], shared_raw[:, 0, :], up_hi[:, 0, :].bitcast(fp32),
                                            ALU.subtract)
                    nc.gpsimd.tensor_tensor(down_lo[:, 0, :], shared_raw[:, 1, :], down_hi[:, 0, :].bitcast(fp32),
                                            ALU.subtract).then_inc(w_lo, 1)
                else:
                    lo, hi = (up_lo, up_hi) if (k - 1) % 2 == 0 else (down_lo, down_hi)
                    c0 = 1 + (k - 1) // 2 * PIECE
                    nc.gpsimd.tensor_tensor(
                        lo[:, c0:c0 + PIECE, :],
                        stage[:, (k - 1) % STAGES].rearrange("p (c m) -> p c m", m=P),
                        hi[:, c0:c0 + PIECE, :].bitcast(fp32), ALU.subtract).then_inc(w_lo, 1)
                if k == 2 * NP - 2:
                    state_out(0)

            def lo_part(g, ch):
                pool.wait_ge(hi_done, chunks(g, ch))
                nc.gpsimd.tensor_tensor(g_lo[:, ch % RING], g_ring[:, ch % RING],
                                        g_hi[:, ch % RING].bitcast(fp32), ALU.subtract).then_inc(lo_done, 1)

            for ch in range(PARTS):
                lo_part(0, ch)
            def turn(g, states):
                for j in range(TURN, NC):
                    lo_part(*at(g, j + PARTS))
                    if states and j == 27:
                        state_out(g + 2)
                for j in range(TURN):
                    lo_part(g + 1, j + PARTS)

            for j in range(TURN):
                lo_part(0, j + PARTS)
                if j == 1:
                    state_out(1)
            with pool.Fori(0, G - 2) as g:
                turn(g, True)
            turn(G - 2, False)
            for j in range(TURN, NC - PARTS):
                lo_part(G - 1, j + PARTS)

        @block.scalar
        def _(act):
            def mod_of(row, g, half):
                return mod[:, row, bass.ds(2 * g + half, 1)]

            def modulate(dst, src, scale_row, bias_row, g):
                for half in range(2):
                    cols = slice(half * S, (half + 1) * S)
                    src_ps = src[half]
                    if bias_row is None:
                        last = nc.scalar.activation(dst[:, cols], src_ps[:, cols], ACT.Copy,
                                                    scale=mod_of(scale_row, g, half))
                    else:
                        last = nc.scalar.activation(dst[:, cols], src_ps[:, cols], ACT.Identity,
                                                    scale=mod_of(scale_row, g, half), bias=mod_of(bias_row, g, half))
                return last

            def normalise1(g):
                for t in range(TL):
                    last = nc.scalar.activation(xn1[:, t], x_sb[:, g, t], ACT.Identity, scale=ln1[:, 0, g, t:t + 1],
                                                bias=ln1[:, 1, g, t:t + 1])
                last.then_inc(xn1_done, 1)

            def norm1(g):
                act.wait_ge(xn1_ps, g + 1)
                modulate(h1T, (T_ps, T_ps), CA, SA, g).then_inc(h1_done, 1)

            def step_size(g):
                act.wait_ge(d_ps, g + 1)
                nc.scalar.activation(sp[:, 1], T_ps[:, 0:TL], ACT.Abs, bias=bd_sb[:, 0:1]).then_inc(z_done, 1)
                nc.scalar.activation(sp[:, 0], T_ps[:, 0:TL], ACT.Identity, bias=bd_sb[:, 0:1])
                act.wait_ge(z_done, g + 1)
                nc.scalar.activation(sp[:, 2], sp[:, 1], ACT.Silu, scale=-1.0,
                                     bias=minus_one[:, 0:1]).then_inc(sps_done, 1)

            def gate1(g):
                act.wait_ge(y_ps, g + 1)
                modulate(uT, (T_ps, Q_ps), GA, BOGA, g).then_inc(u_done, 1)

            def normalise2(g):
                act.wait_ge(ln2_done, g + 1)
                nc.scalar.copy(act_pad[:], minus_one[:])
                for t in range(TL):
                    last = nc.scalar.activation(xn2[:, t], x_sb[:, g, t], ACT.Identity, scale=ln2[:, 0, t:t + 1],
                                                bias=ln2[:, 1, t:t + 1])
                last.then_inc(xn2_done, 1)

            def norm2(g):
                act.wait_ge(xn2_ps, g + 1)
                modulate(h2T, (T_ps, T_ps), CB, SB, g).then_inc(h2_done, 1)

            def router(g):
                act.wait_ge(aff_ps, g + 1)
                q = Q_ps[:, 0:TL * E].rearrange("p (t e) -> p t e", e=E)
                nc.scalar.activation(aff[:], q, ACT.Copy).then_inc(aff_done, 1)
                nc.scalar.activation(az[:], q, ACT.Abs).then_inc(az_done, 1)
                act.wait_ge(az_done, g + 1)
                nc.scalar.activation(sz[:], az[:], ACT.Silu, scale=-1.0, bias=minus_one[:, 0:1]).then_inc(sz_done, 1)

            def hand_over_tokens(g):
                act.wait_ge(h2_done, g + 1)
                need(act, up_done, chunks(g - 1, NC - 1))
                nc.scalar.copy(h2_hi[:], h2T[:]).then_inc(h2hi_done, 1)

            def hand_over_weights(g):
                act.wait_ge(cwT_ps, g + 1)
                need(act, bc_done, routed(g - 1, NR))
                nc.scalar.copy(cw_T[:], T_ps[:]).then_inc(cwT_done, 1)

            def silu_part(g, ch):
                act.wait_ge(up_done, chunks(g, ch))
                if ch == 0:
                    need(act, lo_done, chunks(g - 1, NC - RING))
                    nc.scalar.activation(g_ring[:, 0], up_ps[0][:], ACT.Silu).then_inc(s_done, 1)
                else:
                    need(act, g_done, routed(g, ch - RING))
                    nc.scalar.activation(s_ring[:, ch % RING], up_ps[ch % RING][:], ACT.Silu).then_inc(s_done, 1)

            def hi_part(g, ch):
                if ch == 0:
                    act.wait_ge(s_done, chunks(g, ch))
                else:
                    act.wait_ge(g_done, routed(g, ch))
                need(act, down_done, chunks(g, ch - RING))
                nc.scalar.copy(g_hi[:, ch % RING], g_ring[:, ch % RING]).then_inc(hi_done, 1)

            def step(g, j):
                silu_part(*at(g, j + UP))
                hi_part(*at(g, j + PARTS))

            def finish(g):
                act.wait_ge(down_done, chunks(g, NC - 1))
                modulate(fT, (down_ps, down_ps), GB, None, g).then_inc(f_done, 1)

            act.wait_ge(c_in, 16)
            nc.scalar.activation(cs_sb[:], c_sb[:], ACT.Silu).then_inc(cs_done, 1)
            act.wait_ge(both_done, 1)
            nc.scalar.copy(sel[:], both[:].unsqueeze(2).broadcast_to([P, E, F])).then_inc(sel_done, 1)
            act.wait_ge(shared_in, 32)
            nc.scalar.copy(up_hi[:, 0, :], shared_raw[:, 0, :]).then_inc(w_hi, 1)
            nc.scalar.copy(down_hi[:, 0, :], shared_raw[:, 1, :]).then_inc(w_hi, 1)

            def split(k):
                act.wait_ge(piece_in[k], 32)
                hi = up_hi if k % 2 == 0 else down_hi
                c0 = 1 + k // 2 * PIECE
                nc.scalar.copy(hi[:, c0:c0 + PIECE, :],
                               stage[:, k % STAGES].rearrange("p (c m) -> p c m", m=P)).then_inc(w_hi, 1)

            act.wait_ge(rs_first, 1)
            normalise1(0)
            split(0)
            split(1)
            act.wait_ge(mod_done, 1)
            norm1(0)
            split(2)
            act.wait_ge(vec_in, 16 * 8)
            step_size(0)
            split(3)
            for k in range(4, 2 * NP):
                split(k)
            gate1(0)
            normalise2(0)
            norm2(0)
            router(0)
            hand_over_tokens(0)
            act.wait_ge(ln1_done, 1)
            normalise1(1)
            norm1(1)
            step_size(1)
            for ch in range(PARTS):
                silu_part(0, ch)
            silu_part(0, PARTS)
            hi_part(0, 0)
            hand_over_weights(0)
            for ch in range(PARTS + 1, LAG):
                silu_part(0, ch)
                hi_part(0, ch - PARTS)

            def turn(g, states):
                for j in range(TURN, NC):
                    step(g, j)
                    if j == 4:
                        gate1(g + 1)
                    if j == 7:
                        normalise2(g + 1)
                    if j == 8:
                        norm2(g + 1)
                    if j == 10:
                        router(g + 1)
                    if states and j == 12:
                        normalise1(g + 2)
                    if states and j == 14:
                        norm1(g + 2)
                    if states and j == 16:
                        step_size(g + 2)
                    if j == NC - LAG - 1:
                        hand_over_tokens(g + 1)
                    if j == NC - LAG:
                        hand_over_weights(g + 1)
                finish(g)
                for j in range(TURN):
                    step(g + 1, j)

            for j in range(TURN):
                step(0, j)
            with act.Fori(0, G - 2) as g:
                turn(g, True)
            turn(G - 2, False)
            for j in range(TURN, NC - UP):
                step(G - 1, j)
            for j in range(NC - UP, NC - PARTS):
                hi_part(G - 1, j + PARTS)
            finish(G - 1)

        @block.vector
        def _(dve):
            DVE_LINKS = 54
            chain = {"base": 0, "n": 0}

            def link(ins):
                chain["n"] += 1
                ins.then_inc(dve_own, 1)
                dve.wait_ge(dve_own, chain["base"] + chain["n"])

            def settle():
                dve.wait_ge(dve_own, chain["base"] + chain["n"])

            def mark(ins):
                chain["n"] += 1
                ins.then_inc(dve_own, 1)

            def atanh_of(t, p, s):
                link(nc.vector.tensor_tensor(t, s, s, ALU.mult))
                link(nc.vector.tensor_scalar(p, t, ATANH_D[3], None, ALU.mult))
                for k in (2, 1, 0):
                    link(nc.vector.scalar_tensor_tensor(p, p, ATANH_D[k], t, ALU.add, ALU.mult))
                link(nc.vector.scalar_tensor_tensor(p, p, 1.0, s, ALU.add, ALU.mult))

            def deviations(mean, var, v, a, out):
                y = out[0]
                link(nc.vector.tensor_scalar(v, var, LN_EPS, None, ALU.add))
                link(nc.vector.tensor_scalar(y.bitcast(i32), v.bitcast(i32), -0.5, RSQRT_GUESS, ALU.mult, ALU.add))
                for _ in range(RSQRT_STEPS):
                    link(nc.vector.tensor_tensor(a, y, y, ALU.mult))
                    link(nc.vector.scalar_tensor_tensor(a, a, -0.5, v, ALU.mult, ALU.mult))
                    link(nc.vector.scalar_tensor_tensor(y, a, 1.5, y, ALU.add, ALU.mult))
                return nc.vector.scalar_tensor_tensor(out[1], mean, -1.0, y, ALU.mult, ALU.mult)

            def moments(g, dst):
                for t in range(TL):
                    last = nc.vector.bn_stats(stats[:, t], x_sb[:, g, t])
                link(last)
                nc.vector.memset(pad[:], 0.0)
                for t in range(TL):
                    last = nc.vector.bn_aggr(dst[:, t], stats[:, t])
                return last

            def step_size_a(g):
                dve.wait_ge(sps_done, g + 1)
                dve.wait_ge(z_done, g + 1)
                nc.vector.tensor_scalar(sp[:, 3], sp[:, 0], 0.0, None, ALU.max)
                link(nc.vector.scalar_tensor_tensor(sp[:, 4], sp[:, 1], 1.0, sp[:, 2], ALU.add, ALU.add))
                link(nc.vector.scalar_tensor_tensor(sp[:, 4], sp[:, 2], -EULER / 2, sp[:, 4], ALU.mult, ALU.add))
                link(nc.vector.reciprocal(sp[:, 4], sp[:, 4]))
                mark(nc.vector.scalar_tensor_tensor(sp[:, 6], sp[:, 2], -EULER / 2, sp[:, 4], ALU.mult, ALU.mult))

            def step_size_b(g):
                settle()
                atanh_of(sp[:, 7], sp[:, 4], sp[:, 6])
                nc.vector.scalar_tensor_tensor(
                    delta_b[:], sp[:, 4].unsqueeze(2).broadcast_to([P, TL, N]), 2.0,
                    sp[:, 3].unsqueeze(2).broadcast_to([P, TL, N]), ALU.mult, ALU.add).then_inc(delta_done, 1)

            def decay_a(g):
                dve.wait_ge(delta_ps, g + 1)
                link(nc.vector.tensor_scalar(u_sb[:], Q_ps[:, S:2 * S], A_sb[:, 0:1], U_LEAST, ALU.mult, ALU.max))
                link(nc.vector.tensor_scalar(n_sb[:], u_sb[:], LOG2E, MAGIC, ALU.mult, ALU.add))
                mark(nc.vector.tensor_scalar(n_sb[:], n_sb[:], -MAGIC, None, ALU.add))

            def decay_b(g):
                settle()
                mark(nc.vector.scalar_tensor_tensor(u_sb[:], n_sb[:], -LN2, u_sb[:], ALU.mult, ALU.add))
                nc.vector.tensor_scalar(pow2[:], n_sb[:], MANT, 127 * MANT, ALU.mult, ALU.add)
                settle()
                link(nc.vector.tensor_scalar(p_sb[:], u_sb[:], EXP_C[4], EXP_C[3], ALU.mult, ALU.add))
                mark(nc.vector.tensor_tensor(p_sb[:], p_sb[:], u_sb[:], ALU.mult))

            def decay_c(g):
                settle()
                for k in (2, 1):
                    link(nc.vector.scalar_tensor_tensor(p_sb[:], p_sb[:], EXP_C[k], u_sb[:], ALU.add, ALU.mult))
                mark(nc.vector.scalar_tensor_tensor(p_sb[:], p_sb[:], EXP_C[0], u_sb[:], ALU.add, ALU.mult))

            def decay_d(g):
                settle()
                link(nc.vector.scalar_tensor_tensor(p_sb[:], p_sb[:], 1.0, u_sb[:], ALU.add, ALU.mult))
                link(nc.vector.scalar_tensor_tensor(dA[:], p_sb[:], 1.0, pow2[:].bitcast(fp32), ALU.add, ALU.mult))
                nc.vector.memset(Ct[:, 0:1], 1.0)
                mark(nc.vector.tensor_tensor_scan(Ct[:, 1:S], dA[:, 0:S - 1], zeros[:, 0:S - 1], 1.0,
                                                  ALU.mult, ALU.add))

            def state_a(g):
                dve.wait_ge(b_ps, g + 1)
                nc.vector.tensor_scalar(p_sb[:], dA[:], -1.0, rA[:, 0:1], ALU.add, ALU.mult)
                settle()
                mark(nc.vector.tensor_scalar(u_sb[:], Ct[:], SSM_EPS, None, ALU.add))
                settle()
                mark(nc.vector.scalar_tensor_tensor(dB[:], Q_ps[:, 0:S], bB_sb[:, 0:1], p_sb[:], ALU.add, ALU.mult))

            def state_b(g):
                settle()
                mark(nc.vector.reciprocal(u_sb[:], u_sb[:]))

            def state_c(g):
                settle()
                link(nc.vector.tensor_tensor(dB[:], dB[:], u_sb[:], ALU.mult))
                nc.vector.tensor_tensor_scan(s_sum[:], dB[:], zeros[:], 0.0, ALU.add, ALU.add).then_inc(sum_done, 1)

            def residual1(g):
                dve.wait_ge(u_ps, g + 1)
                mark(nc.vector.tensor_tensor(x_sb[:, g].rearrange("p t d -> p (t d)"),
                                             x_sb[:, g].rearrange("p t d -> p (t d)"), Q_ps[:], ALU.add))

            def moments2(g):
                settle()
                nc.vector.memset(pad[:], 0.0)
                mark(moments(g, mv))

            def deviations2(g):
                settle()
                deviations(mv[:, :, 0], mv[:, :, 1], rs[:, 0], rs[:, 1],
                           (ln2[:, 0], ln2[:, 1])).then_inc(ln2_done, 1)

            def router_top(g):
                dve.wait_ge(aff_done, g + 1)
                link(nc.vector.tensor_tensor(biased[:], aff[:], bias_sb[:].unsqueeze(1).broadcast_to([P, TL, E]), ALU.add))
                nc.vector.memset(pad[:], 0.0)
                for t in range(TL):
                    last = nc.vector.max(top[:, t], biased[:, t])
                mark(last)

            def router_chosen(g):
                settle()
                nc.vector.memset(pad[:], 0.0)
                for t in range(TL):
                    last = nc.vector.match_replace(left[:, t], top[:, t], biased[:, t], LOWEST)
                mark(last)

            def sigmoid_a(g):
                dve.wait_ge(sz_done, g + 1)
                dve.wait_ge(az_done, g + 1)
                link(nc.vector.scalar_tensor_tensor(az[:], az[:], 1.0, sz[:], ALU.add, ALU.add))
                mark(nc.vector.scalar_tensor_tensor(aff[:], aff[:], 0.0, az[:], ALU.is_ge, ALU.mult))
                nc.vector.scalar_tensor_tensor(ez[:], sz[:], -EULER, az[:], ALU.mult, ALU.add)
                settle()
                mark(nc.vector.scalar_tensor_tensor(aff[:], sz[:], -EULER, aff[:], ALU.mult, ALU.max))

            def sigmoid_b(g):
                settle()
                mark(nc.vector.reciprocal(ez[:], ez[:]))

            def router_sum(g):
                settle()
                link(nc.vector.scalar_tensor_tensor(aff[:], left[:], LOWEST, aff[:], ALU.is_equal, ALU.mult))
                link(nc.vector.tensor_tensor(ez[:], aff[:], ez[:], ALU.mult))
                mark(nc.vector.tensor_reduce(wsum[:], ez[:], AX.X, ALU.add))

            def router_out(g):
                settle()
                link(nc.vector.tensor_scalar(wsum[:], wsum[:], SUM_EPS, None, ALU.add))
                link(nc.vector.reciprocal(wsum[:], wsum[:]))
                link(nc.vector.tensor_tensor(ez[:], ez[:], wsum[:].unsqueeze(2).broadcast_to([P, TL, E]), ALU.mult))
                link(nc.vector.tensor_copy(cw_hl[:, :, 0], ez[:]))
                nc.vector.tensor_tensor(cw_hl[:, :, 1], ez[:], cw_hl[:, :, 0].bitcast(fp32),
                                        ALU.subtract).then_inc(cw_done, 1)

            def hand_over(g):
                dve.wait_ge(h2hi_done, g + 1)
                nc.vector.tensor_tensor(h2_lo[:], h2T[:], h2_hi[:].bitcast(fp32), ALU.subtract).then_inc(h2lo_done, 1)

            def weigh(g, ch):
                if ch == 0:
                    return
                dve.wait_ge(s_done, chunks(g, ch))
                dve.wait_ge(bc_done, routed(g, ch))
                need(dve, lo_done, chunks(g, ch - RING))
                nc.vector.tensor_tensor(g_ring[:, ch % RING], s_ring[:, ch % RING], cw_ps[ch % 2][:],
                                        ALU.mult).then_inc(g_done, 1)

            def finish(g):
                dve.wait_ge(f_ps, g + 1)
                dve.wait_ge(out_done, 16 * (g + 1))
                nc.vector.tensor_tensor(out_sb[:].rearrange("p t d -> p (t d)"),
                                        x_sb[:, g].rearrange("p t d -> p (t d)"), T_ps[:], ALU.add).then_inc(out_ready, 1)

            def state_decay():
                W = lambda i: wk[:, i:i + 1]
                LN2_HI, LN2_LO = 0.693359375, -2.12194440e-4
                link(nc.vector.scalar_tensor_tensor(W(1), W(0), -1.0, W(0), ALU.mult, ALU.max))
                link(nc.vector.tensor_scalar(W(1), W(1), -U_LEAST, None, ALU.min))
                link(nc.vector.tensor_scalar(W(2), W(1), LOG2E, MAGIC, ALU.mult, ALU.add))
                link(nc.vector.tensor_scalar(W(2), W(2), -MAGIC, None, ALU.add))
                link(nc.vector.scalar_tensor_tensor(W(3), W(2), -LN2_HI, W(1), ALU.mult, ALU.add))
                link(nc.vector.scalar_tensor_tensor(W(3), W(2), -LN2_LO, W(3), ALU.mult, ALU.add))
                link(nc.vector.tensor_scalar(W(3), W(3), -1.0, None, ALU.mult))
                link(nc.vector.tensor_scalar(W(4), W(3), EXP_C[4], EXP_C[3], ALU.mult, ALU.add))
                link(nc.vector.tensor_tensor(W(4), W(4), W(3), ALU.mult))
                for add in (EXP_C[2], EXP_C[1], EXP_C[0], 1.0):
                    link(nc.vector.scalar_tensor_tensor(W(4), W(4), add, W(3), ALU.add, ALU.mult))
                link(nc.vector.tensor_scalar(wki[:], W(2), -MANT, 127 * MANT, ALU.mult, ALU.add))
                link(nc.vector.scalar_tensor_tensor(W(5), W(4), 1.0, wki[:].bitcast(fp32), ALU.add, ALU.mult))
                link(nc.vector.tensor_scalar(W(7), W(5), 2.0, None, ALU.add))
                link(nc.vector.reciprocal(W(7), W(7)))
                link(nc.vector.tensor_tensor(W(8), W(5), W(7), ALU.mult))
                atanh_of(W(9), W(10), W(8))
                link(nc.vector.tensor_scalar(W(6), W(0), 0.0, -1.0, ALU.max, ALU.mult))
                link(nc.vector.scalar_tensor_tensor(A_sb[:], W(10), -2.0, W(6), ALU.mult, ALU.add))
                link(nc.vector.tensor_scalar(rA[:], A_sb[:], SSM_EPS, None, ALU.add))
                link(nc.vector.reciprocal(rA[:], rA[:]))

            dve.sem_inc(out_ready, 1)
            dve.wait_ge(ident_done, 3)
            nc.vector.tensor_tensor(both[:], ident[:, 0:E], ident[:, E:2 * E], ALU.add).then_inc(both_done, 1)
            dve.wait_ge(x_in[0], 16)
            link(moments(0, mv1[:, 0]))
            deviations(mv1[:, 0, :, 0], mv1[:, 0, :, 1], rs1[:, 0, 0], rs1[:, 1, 0],
                       (ln1[:, 0, 0], ln1[:, 1, 0])).then_inc(rs_first, 1)
            dve.wait_ge(csT_ps, 1)
            nc.vector.tensor_copy(cs_T[:], Q_ps[:, 0:BATCH]).then_inc(csT_done, 1)
            dve.wait_ge(wT_ps, 1)
            nc.vector.tensor_copy(WB_T[:], T_ps[:, 128:128 + N])
            nc.vector.tensor_copy(Wo_T[:], T_ps[:, 256:256 + D])
            nc.vector.tensor_copy(cent_T[:], T_ps[:, 384:384 + E]).then_inc(wT_done, 1)
            dve.wait_ge(mod_ps, 1)
            dve.wait_ge(vec_in, 16 * 8)
            m = Q_ps[:, 0:6 * BATCH].rearrange("p (r b) -> p r b", b=BATCH)
            link(nc.vector.tensor_copy(mod[:, 0:6], m))
            for r in (CA, CB):
                nc.vector.tensor_scalar(mod[:, r], mod[:, r], 1.0, None, ALU.add)
            for i, r in enumerate((GA, GB)):
                last = nc.vector.tensor_scalar(sgn[:, i], mod[:, r], 0.0, 2.0, ALU.is_ge, ALU.mult)
            link(last)
            for i, r in enumerate((GA, GB)):
                last = nc.vector.tensor_scalar(sgn[:, i], sgn[:, i], -1.0, None, ALU.add)
            link(last)
            for i, r in enumerate((GA, GB)):
                last = nc.vector.scalar_tensor_tensor(mod[:, r], mod[:, r], -1.0, mod[:, r], ALU.mult, ALU.max)
            link(last)
            for i, r in enumerate((GA, GB)):
                last = nc.vector.scalar_tensor_tensor(mod[:, r], mod[:, r], 0.25, sgn[:, i], ALU.max, ALU.mult)
            link(last)
            nc.vector.tensor_scalar(mod[:, BOGA], mod[:, GA], bo_sb[:, 0:1], None, ALU.mult).then_inc(mod_done, 1)
            state_decay()
            step_size_a(0)
            step_size_b(0)
            dve.wait_ge(x_in[1], 16)
            link(moments(1, mv1[:, 1]))
            decay_a(0)
            decay_b(0)
            decay_c(0)
            decay_d(0)
            state_a(0)
            state_b(0)
            state_c(0)
            for k in (2, 3, 4):
                dve.wait_ge(x_in[k], 16)
                link(moments(k, mv1[:, k]))
            residual1(0)
            moments2(0)
            deviations2(0)
            for k in (5, 6, 7):
                dve.wait_ge(x_in[k], 16)
                link(moments(k, mv1[:, k]))
            deviations(mv1[:, 1:, :, 0], mv1[:, 1:, :, 1], rs1[:, 0, 1:], rs1[:, 1, 1:],
                       (ln1[:, 0, 1:], ln1[:, 1, 1:])).then_inc(ln1_done, 1)
            router_top(0)
            router_chosen(0)
            sigmoid_a(0)
            hand_over(0)
            sigmoid_b(0)
            router_sum(0)
            router_out(0)
            def turn(g, states):
                for j in range(TURN, NC):
                    weigh(*at(g, j + WEIGH))
                    if j == 5:
                        residual1(g + 1)
                        moments2(g + 1)
                    if j == 6:
                        deviations2(g + 1)
                    if j == 10:
                        router_top(g + 1)
                    if j == 11:
                        router_chosen(g + 1)
                    if j == 12:
                        sigmoid_a(g + 1)
                    if j == 13:
                        sigmoid_b(g + 1)
                    if j == 15:
                        router_sum(g + 1)
                    if j == 16:
                        router_out(g + 1)
                    if states and j == 17:
                        step_size_a(g + 2)
                    if states and j == 18:
                        step_size_b(g + 2)
                    if states and j == 20:
                        decay_a(g + 2)
                    if states and j == 21:
                        decay_b(g + 2)
                    if states and j == 22:
                        decay_c(g + 2)
                    if states and j == 23:
                        decay_d(g + 2)
                    if states and j == 24:
                        state_a(g + 2)
                    if states and j == 25:
                        state_b(g + 2)
                    if states and j == 27:
                        state_c(g + 2)
                    if j == NC - LAG - 1:
                        hand_over(g + 1)
                for j in range(TURN):
                    weigh(g + 1, j + WEIGH)
                    if j == 2:
                        finish(g)

            step_size_a(1)
            step_size_b(1)
            weigh(0, 1)
            decay_a(1)
            weigh(0, 2)
            decay_b(1)
            weigh(0, 3)
            decay_c(1)
            weigh(0, 4)
            decay_d(1)
            state_a(1)
            weigh(0, 5)
            state_b(1)
            state_c(1)
            setup_links = chain["n"]
            with dve.Fori(0, G - 2) as g:
                chain["base"], chain["n"] = g * DVE_LINKS + setup_links, 0
                turn(g, True)
                assert chain["n"] == DVE_LINKS, chain["n"]
            chain["base"], chain["n"] = (G - 2) * DVE_LINKS + setup_links, 0
            turn(G - 2, False)
            for j in range(TURN, NC - WEIGH):
                weigh(G - 1, j + WEIGH)
            finish(G - 1)

        @block.tensor
        def _(pe):
            def transpose_tiles(dst, src):
                for t in range(TL):
                    last = nc.tensor.transpose(dst[:, t * P:(t + 1) * P], src(t), ident[:])
                return last

            def norm1(g):
                pe.wait_ge(xn1_done, g + 1)
                transpose_tiles(T_ps, lambda t: xn1[:, t]).then_inc(xn1_ps, 1)

            def project(g):
                pe.wait_ge(h1_done, g + 1)
                for t in range(TL):
                    last = nc.tensor.matmul(T_ps[:, t:t + 1], h1T[:, t * P:(t + 1) * P], Wd_sb[:], start=True, stop=True)
                last.then_inc(d_ps, 1)
                for half in range(2):
                    last = nc.tensor.matmul(Q_ps[half * N:(half + 1) * N, 0:S], WB_T[:],
                                            h1T[:, half * S:(half + 1) * S], start=True, stop=True)
                last.then_inc(b_ps, 1)

            def spread(g):
                pe.wait_ge(delta_done, g + 1)
                for t in range(TL):
                    half, col = t // (TL // 2), S + t % (TL // 2) * P
                    last = nc.tensor.matmul(Q_ps[half * N:(half + 1) * N, col:col + P], delta_b[:, t], ident[:],
                                            start=True, stop=True)
                last.then_inc(delta_ps, 1)

            def state_out(g):
                pe.wait_ge(y_done, g + 1)
                need(pe, out_ready, g)
                for half in range(2):
                    rows = slice(half * N, (half + 1) * N)
                    last = nc.tensor.matmul((T_ps, Q_ps)[half][:, half * S:(half + 1) * S], Wo_T[rows, :], y_sb[rows, :],
                                            start=True, stop=True)
                last.then_inc(y_ps, 1)

            def residual1(g):
                pe.wait_ge(u_done, g + 1)
                transpose_tiles(Q_ps, lambda t: uT[:, t * P:(t + 1) * P]).then_inc(u_ps, 1)

            def norm2(g):
                pe.wait_ge(xn2_done, g + 1)
                transpose_tiles(T_ps, lambda t: xn2[:, t]).then_inc(xn2_ps, 1)

            def affinities(g):
                pe.wait_ge(h2_done, g + 1)
                for t in range(TL):
                    last = nc.tensor.matmul(Q_ps[:, t * E:(t + 1) * E], h2T[:, t * P:(t + 1) * P], cent_T[:],
                                            start=True, stop=True)
                last.then_inc(aff_ps, 1)

            def route(g, states=True):
                pe.wait_ge(cw_done, g + 1)
                if states:
                    pe.wait_ge(sps_done, g + 2)
                transpose_tiles(T_ps, lambda t: cw_hl[:, t].rearrange("p h e -> p (h e)").bitcast(fp32)).then_inc(cwT_ps, 1)

            def up(g, ch):
                if ch == 0:
                    pe.wait_ge(h2hi_done, g + 1)
                    need(pe, s_done, chunks(g - 1, NC - RING))
                else:
                    need(pe, s_done, chunks(g, ch - RING))
                u = up_ps[ch % RING]
                nc.tensor.matmul(u[:], up_lo[:, ch, :], h2_hi[:], start=True, stop=False)
                if ch == 0:
                    nc.tensor.matmul(u[:], up_hi[:, ch, :], h2_hi[:], start=False, stop=False)
                    pe.wait_ge(h2lo_done, g + 1)
                    nc.tensor.matmul(u[:], up_hi[:, ch, :], h2_lo[:], start=False, stop=True).then_inc(up_done, 1)
                    return
                nc.tensor.matmul(u[:], up_hi[:, ch, :], h2_hi[:], start=False, stop=False)
                nc.tensor.matmul(u[:], up_hi[:, ch, :], h2_lo[:], start=False, stop=True).then_inc(up_done, 1)

            def weights(g, ch):
                if ch == 0:
                    return
                if ch == 1:
                    pe.wait_ge(cwT_done, g + 1)
                need(pe, g_done, routed(g, ch - 2))
                nc.tensor.matmul(cw_ps[ch % 2][:], sel[:, 2 * ch - 2:2 * ch, :].rearrange("p e f -> p (e f)"), cw_T[:],
                                 start=True, stop=True).then_inc(bc_done, 1)

            def down(g, ch):
                if ch == 0:
                    need(pe, f_done, g)
                pe.wait_ge(hi_done, chunks(g, ch))
                nc.tensor.matmul(down_ps[:], down_lo[:, ch, :], g_hi[:, ch % RING], start=ch == 0, stop=False)
                nc.tensor.matmul(down_ps[:], down_hi[:, ch, :], g_hi[:, ch % RING], start=False, stop=False)
                pe.wait_ge(lo_done, chunks(g, ch))
                nc.tensor.matmul(down_ps[:], down_hi[:, ch, :], g_lo[:, ch % RING], start=False,
                                 stop=ch == NC - 1).then_inc(down_done, 1)

            def finish(g):
                pe.wait_ge(f_done, g + 1)
                transpose_tiles(T_ps, lambda t: fT[:, t * P:(t + 1) * P]).then_inc(f_ps, 1)

            pe.wait_ge(ident_done, 1)
            pe.wait_ge(cs_done, 1)
            nc.tensor.transpose(Q_ps[:, 0:BATCH], cs_sb[:], ident[0:BATCH, 0:BATCH]).then_inc(csT_ps, 1)
            pe.wait_ge(WB_in, 16)
            nc.tensor.transpose(T_ps[:, 128:128 + N], WB_sb[:], ident[0:N, 0:N])
            pe.wait_ge(Wo_in, 32)
            nc.tensor.transpose(T_ps[:, 256:256 + D], Wo_sb[:].rearrange("d h n -> d (h n)"), ident[:])
            pe.wait_ge(cent_in, 16)
            nc.tensor.transpose(T_ps[:, 384:384 + E], cent_sb[:], ident[0:E, 0:E]).then_inc(wT_ps, 1)
            pe.wait_ge(csT_done, 1)
            pe.wait_ge(wmod_in, 16)
            for r in range(6):
                last = nc.tensor.matmul(Q_ps[:, r * BATCH:(r + 1) * BATCH], wmod_sb[:, r * D:(r + 1) * D], cs_T[:],
                                        start=True, stop=True)
            last.then_inc(mod_ps, 1)
            pe.wait_ge(wT_done, 1)
            norm1(0)
            pe.wait_ge(mod_done, 1)
            project(0)
            spread(0)
            state_out(0)
            residual1(0)
            norm2(0)
            affinities(0)
            pe.wait_ge(ln1_done, 1)
            norm1(1)
            project(1)
            pe.wait_ge(w_lo, 2 * NP + 1)
            pe.wait_ge(sel_done, 1)
            up(0, 0)
            up(0, 1)
            up(0, 2)
            route(0)
            weights(0, 1)
            up(0, 3)
            weights(0, 2)

            def turn(g, states):
                for j in range(TURN, NC):
                    if j + UP == NC:
                        weights(*at(g, j + WEIGH))
                    up(*at(g, j + UP))
                    if j + UP != NC:
                        weights(*at(g, j + WEIGH))
                    if j == 3:
                        state_out(g + 1)
                    if j == 5:
                        residual1(g + 1)
                    if j == 8:
                        norm2(g + 1)
                    if j == 9:
                        affinities(g + 1)
                    if states and j == 13:
                        norm1(g + 2)
                    if states and j == 15:
                        project(g + 2)
                    if j == 19:
                        route(g + 1, states)
                    if states and j == 20:
                        spread(g + 2)
                    down(g, j)
                for j in range(TURN):
                    up(g + 1, j + UP)
                    weights(g + 1, j + WEIGH)
                    if j == 1:
                        finish(g)
                    down(g + 1, j)

            for j in range(TURN):
                up(0, j + UP)
                weights(0, j + WEIGH)
                if j == 0:
                    spread(1)
                down(0, j)
            with pe.Fori(0, G - 2) as g:
                turn(g, True)
            turn(G - 2, False)
            for j in range(TURN, NC - UP):
                up(G - 1, j + UP)
                weights(G - 1, j + WEIGH)
                down(G - 1, j)
            for j in range(NC - UP, NC):
                if j + WEIGH < NC:
                    weights(G - 1, j + WEIGH)
                down(G - 1, j)
            finish(G - 1)


_INS = ["L0_attn_x", "L0_attn_A_log", "L0_attn_WB", "L0_attn_bB", "L0_attn_Wd", "L0_attn_bd", "L0_attn_Wo",
        "L0_attn_bo", "L0_ffn_centroids", "L0_ffn_expert_biases", "L0_ffn_Ws_up", "L0_ffn_Ws_down",
        "L0_ffn_W_up", "L0_ffn_W_down", "L0_c", "L0_wmod"]


def kernel(**inputs):
    import numpy as _np
    import concourse.bacc as _bacc
    from concourse import mybir as _mybir
    from concourse.bass_utils import run_bass_kernel_spmd as _run

    nc = _bacc.Bacc("TRN2", target_bir_lowering=False, num_devices=1)
    arrays, args = {}, []
    for name in _INS:
        a = _np.ascontiguousarray(inputs[name])
        arrays[f"in_{name}"] = a
        args.append(nc.dram_tensor(f"in_{name}", a.shape, _mybir.dt.from_np(a.dtype), kind="ExternalInput").ap())
    shape = inputs["L0_attn_x"].shape
    args.append(nc.dram_tensor("out_0", shape, _mybir.dt.float32, kind="ExternalOutput").ap())
    adaln_ssm_moe_kernel(nc, *args)
    r = _run(nc, [arrays], core_ids=[0])
    return r.results[0]["out_0"]
```

```python
import concourse.bass as bass
from concourse import mybir
from contextlib import ExitStack


def adaln_ssm_moe_kernel(nc, x, A_log, WB, bB, Wd, bd, Wo, bo, centroids, expert_biases,
                         Ws_up, Ws_down, W_up, W_down, c, wmod, out):
    fp32 = mybir.dt.float32
    r32 = mybir.dt.float32r
    i32 = mybir.dt.int32
    ALU = mybir.AluOpType
    ACT = mybir.ActivationFunctionType
    AX = mybir.AxisListType

    P = 128
    BATCH, S, D = x.shape
    N = A_log.shape[0]
    E, _, F = W_up.shape
    GT = 2 * S
    G = BATCH * S // GT
    TL = GT // P
    NC = E * F // P + 1
    NR = NC - 1
    RING = 3
    LAG = 4
    TURN = 3
    TOPK = 8
    LN_EPS, SSM_EPS, SUM_EPS = 1e-5, 1e-6, 1e-8
    EXP_C = (0.5000000095, 0.1666651860, 0.0416662051, 0.0083689186, 0.0013950541)
    LOG2E, LN2, MAGIC = 1.4426950408889634, 0.6931471805599453, 12582912.0
    MANT, U_LEAST = 8388608.0, -87.0
    ATANH_D = (0.3333320657, 0.2001084955, 0.1399957025, 0.1401223059)
    LOWEST = -3.0e38
    EULER = 2.718281828459045
    RSQRT_GUESS, RSQRT_STEPS = float(0x5F3759DF), 3
    SA, CA, GA, SB, CB, GB, BOGA = range(7)
    PIECE = 8
    NP = NR // PIECE
    STAGES = 4
    assert D == P and 2 * N == P and 2 * F == P and NC % RING == 0 and NR % 2 == 0 and NR % PIECE == 0

    x_v = x.rearrange("b s d -> (b s) d").rearrange("(g t p) d -> g p t d", t=TL, p=P)
    out_v = out.rearrange("b s d -> (b s) d").rearrange("(g t p) d -> g p t d", t=TL, p=P)
    up_v = W_up.rearrange("e d f -> d e f")
    down_v = W_down.rearrange("e f d -> (e f) d").rearrange("(c p) d -> p c d", p=P)

    ctx = ExitStack()
    with ctx:
        def sb(name, shape, dt=fp32):
            return ctx.enter_context(nc.sbuf_tensor(name, shape, dt))

        def sem(name):
            return ctx.enter_context(nc.semaphore(name))

        x_sb = sb("x_sb", [P, G, TL, D])
        ident = sb("ident", [P, P])
        both = sb("both", [P, E])
        sel = sb("sel", [P, E, F], r32)
        stage = sb("stage", [P, STAGES, PIECE * P])
        shared_raw = sb("shared_raw", [P, 2, P])
        up_hi = sb("up_hi", [P, NC, P], r32)
        up_lo = sb("up_lo", [P, NC, P], r32)
        down_hi = sb("down_hi", [P, NC, P], r32)
        down_lo = sb("down_lo", [P, NC, P], r32)
        WB_sb = sb("WB_sb", [N, D])
        Wd_sb = sb("Wd_sb", [D, 1])
        Wo_sb = sb("Wo_sb", [P, 2, N])
        cent_sb = sb("cent_sb", [E, D])
        WB_T = sb("WB_T", [D, N])
        Wo_T = sb("Wo_T", [P, D])
        cent_T = sb("cent_T", [D, E])
        bB_sb = sb("bB_sb", [P, 1])
        bd_sb = sb("bd_sb", [P, 1])
        bo_sb = sb("bo_sb", [D, 1])
        bias_sb = sb("bias_sb", [P, E])
        A_sb = sb("A_sb", [P, 1])
        rA = sb("rA", [P, 1])
        pad = sb("pad", [P, 1])
        minus_one = sb("minus_one", [P, 1])
        wk = sb("wk", [P, 16])
        wki = sb("wki", [P, 1], i32)
        c_sb = sb("c_sb", [BATCH, D])
        cs_sb = sb("cs_sb", [BATCH, D])
        cs_T = sb("cs_T", [D, BATCH])
        wmod_sb = sb("wmod_sb", [D, 6 * D])
        mod = sb("mod", [D, 7, BATCH])
        gate_sign = sb("gate_sign", [D, 2, BATCH])
        gate_size = sb("gate_size", [D, 2, BATCH])
        stats = sb("stats", [P, TL, 6])
        stats1 = sb("stats1", [P, TL, 6])
        mv = sb("mv", [P, TL, 2])
        rs = sb("rs", [P, 2, TL])
        ln2 = sb("ln2", [P, 2, TL])
        mv1 = sb("mv1", [P, G, TL, 2])
        rs1 = sb("rs1", [P, 2, G, TL])
        ln1 = sb("ln1", [P, 2, G, TL])
        xn1 = sb("xn1", [P, TL, D])
        xn2 = sb("xn2", [P, TL, D])
        h1T = sb("h1T", [D, GT])
        sp = sb("sp", [P, 8, TL])
        delta_b = sb("delta_b", [P, TL, N])
        u_sb = sb("u_sb", [P, S])
        n_sb = sb("n_sb", [P, S])
        p_sb = sb("p_sb", [P, S])
        pow2 = sb("pow2", [P, S], i32)
        dA = sb("dA", [P, S])
        Ct = sb("Ct", [P, S])
        dB = sb("dB", [P, S])
        zeros = sb("zeros", [P, S])
        s_sum = sb("s_sum", [P, S])
        y_sb = sb("y_sb", [P, S])
        uT = sb("uT", [D, GT])
        h2T = sb("h2T", [D, GT])
        aff = sb("aff", [P, TL, E])
        biased = sb("biased", [P, TL, E])
        left = sb("left", [P, TL, E])
        top = sb("top", [P, TL, TOPK])
        az = sb("az", [P, TL, E])
        sz = sb("sz", [P, TL, E])
        ez = sb("ez", [P, TL, E])
        wsum = sb("wsum", [P, TL])
        cw_hl = sb("cw_hl", [P, TL, 2, E], r32)
        h2_hi = sb("h2_hi", [D, GT], r32)
        h2_lo = sb("h2_lo", [D, GT], r32)
        cw_T = sb("cw_T", [2 * E, GT], r32)
        s_ring = sb("s_ring", [P, RING, GT])
        g_ring = sb("g_ring", [P, RING, GT])
        g_hi = sb("g_hi", [P, RING, GT], r32)
        g_lo = sb("g_lo", [P, RING, GT], r32)
        fT = sb("fT", [D, GT])
        out_sb = sb("out_sb", [P, TL, D])

        def bank(name):
            return ctx.enter_context(nc.psum_tensor(name, [P, GT], fp32))

        up_ps = [bank(f"up_ps{i}") for i in range(RING)]
        cw_ps = [bank(f"cw_ps{i}") for i in range(2)]
        down_ps = bank("down_ps")
        T_ps = bank("T_ps")
        Q_ps = bank("Q_ps")

        x_in = [sem(f"x_in{i}") for i in range(G)]
        c_in, wmod_in, vec_in, WB_in, Wo_in, cent_in, bd_in, A_in = (sem(n) for n in (
            "c_in", "wmod_in", "vec_in", "WB_in", "Wo_in", "cent_in", "bd_in", "A_in"))
        shared_in = sem("shared_in")
        piece_in = [sem(f"piece_in{i}") for i in range(2 * NP)]
        out_done = sem("out_done")
        ident_done, pool_own, dve_own = (sem(n) for n in ("ident_done", "pool_own", "dve_own"))
        both_done, sel_done = sem("both_done"), sem("sel_done")
        cs_done, csT_ps, csT_done, mod_ps, mod_done, gates_done = (sem(n) for n in (
            "cs_done", "csT_ps", "csT_done", "mod_ps", "mod_done", "gates_done"))
        wT_ps, wT_done = sem("wT_ps"), sem("wT_done")
        ln1_done = sem("ln1_done")
        w_hi, w_lo = sem("w_hi"), sem("w_lo")
        names = ("xn1_done", "xn1_ps", "h1_done", "d_ps", "b_ps", "z_done", "sps_done", "delta_done", "delta_ps",
                 "sum_done", "ss_done", "y_done", "y_ps", "u_done", "u_ps", "xn2_done", "xn2_ps", "h2_done",
                 "aff_ps", "aff_done", "az_done", "sz_done", "cw_done", "cwT_ps", "h2hi_done", "h2lo_done", "cwT_done",
                 "tokens_read", "f_done", "f_ps", "out_ready")
        (xn1_done, xn1_ps, h1_done, d_ps, b_ps, z_done, sps_done, delta_done, delta_ps,
         sum_done, ss_done, y_done, y_ps, u_done, u_ps, xn2_done, xn2_ps, h2_done,
         aff_ps, aff_done, az_done, sz_done, cw_done, cwT_ps, h2hi_done, h2lo_done, cwT_done,
         tokens_read, f_done, f_ps, out_ready) = (sem(n) for n in names)
        up_done, bc_done, s_done, g_done, hi_done, lo_done, down_done = (sem(n) for n in (
            "up_done", "bc_done", "s_done", "g_done", "hi_done", "lo_done", "down_done"))
        shared_lo_done = sem("shared_lo_done")

        def need(eng, s, value):
            if not isinstance(value, int) or value > 0:
                eng.wait_ge(s, value)

        def chunks(g, ch):
            return g * NC + (ch + 1)

        def routed(g, ch):
            return g * NR + ch

        UP, WEIGH, PARTS = LAG, LAG - 1, LAG - 2

        def at(g, i):
            return (g, i) if i < NC else (g + 1, i - NC)

        PE_NEXT = dict(state_out=3, residual1=6, norm2=12, affinities=13, route=23)
        PE_AHEAD = dict(norm1=15, project=18, spread=23)
        PE_FINISH = 33
        ACT_NEXT = dict(gate1=3, norm2=11, router=13, hand_over_weights=28)
        ACT_AHEAD = dict(norm1=15, step_size=18)
        ACT_FINISH = 32
        DVE_NEXT = dict(residual1=6, moments2_a=6, moments2_b=7, deviations2_a=7, deviations2_b=7,
                        deviations2_c=8, normalise2=9, router_top=13, router_chosen=14, sigmoid_a=14,
                        sigmoid_b=15, sigmoid_over1=16, sigmoid_over2=16, router_sum=18, router_scale=18,
                        router_split=19, hand_over=28)
        DVE_AHEAD = dict(normalise1=12, step_size_a=20, step_size_b=20, step_size_c=20, decay_a=22, decay_b=24,
                         decay_c1=25, decay_c2=26, decay_d1=26, decay_d2=27, state_a=30, state_b1=31,
                         state_b2=31, state_c=32)
        DVE_FINISH = 34
        POOL_STATE_OUT = 33
        PE_NEXT_0 = dict(state_out=5, residual1=6, norm2=12, affinities=13, route=22)
        PE_AHEAD_0 = dict(norm1=17, project=19, spread=23)
        ACT_NEXT_0 = dict(gate1=4, norm2=11, router=13, hand_over_weights=28)
        ACT_AHEAD_0 = dict(norm1=16, step_size=19)
        DVE_NEXT_0 = dict(residual1=5, moments2_a=6, moments2_b=6, deviations2_a=7, deviations2_b=8,
                          deviations2_c=8, normalise2=9, router_top=13, router_chosen=14, sigmoid_a=16,
                          sigmoid_b=16, sigmoid_over1=17, sigmoid_over2=17, router_sum=18, router_scale=19,
                          router_split=19, hand_over=27)
        DVE_AHEAD_0 = dict(normalise1=14, step_size_a=20, step_size_b=21, step_size_c=21, decay_a=23,
                           decay_b=23, decay_c1=25, decay_c2=25, decay_d1=26, decay_d2=27, state_a=29,
                           state_b1=30, state_b2=31, state_c=32)
        DVE_MOMENTS_0 = dict(moments5=10, moments6=12, moments7=33, deviations1=35)
        POOL_STATE_OUT_0 = 33

        block = ctx.enter_context(nc.Block())

        @block.sync
        def _(sync):
            sync.sem_inc(out_done, 16)
            sync.dma_start(x_sb[:, 0], x_v[0]).then_inc(x_in[0], 16)
            sync.dma_start(c_sb[:], c).then_inc(c_in, 16)
            sync.dma_start(wmod_sb[:], wmod).then_inc(wmod_in, 16)
            sync.dma_start(WB_sb[:], WB).then_inc(WB_in, 16)
            sync.dma_start(Wd_sb[:], Wd.rearrange("o d -> d o")).then_inc(WB_in, 16)
            sync.dma_start(bd_sb[:], bd.rearrange("(o n) -> o n", o=1).broadcast_to([P, 1])).then_inc(bd_in, 16)
            for h in range(2):
                sync.dma_start(wk[h * N:(h + 1) * N, 0:1], A_log.rearrange("(n o) -> n o", o=1)).then_inc(A_in, 16)
            for h in range(2):
                sync.dma_start(bB_sb[h * N:(h + 1) * N, :], bB.rearrange("(n o) -> n o", o=1)).then_inc(vec_in, 16)
            sync.dma_start(bo_sb[:], bo.rearrange("(d o) -> d o", o=1)).then_inc(vec_in, 16)
            for h in range(2):
                sync.dma_start(Wo_sb[:, h, :], Wo).then_inc(Wo_in, 16)
            sync.dma_start(cent_sb[:], centroids).then_inc(cent_in, 16)
            sync.dma_start(bias_sb[:], expert_biases.rearrange("(o n) -> o n", o=1).broadcast_to([P, E])).then_inc(vec_in, 16)
            for h in range(2):
                sync.dma_start(shared_raw[:, 0, h * F:(h + 1) * F], Ws_up).then_inc(shared_in, 16)
                sync.dma_start(shared_raw[h * F:(h + 1) * F, 1, :], Ws_down).then_inc(shared_in, 16)
            for k in range(2 * NP):
                i = k // 2
                if k >= STAGES:
                    sync.wait_ge(w_lo, k - STAGES + 2)
                if k % 2 == 0:
                    for e0 in range(0, 2 * PIECE, PIECE):
                        sync.dma_start(
                            stage[:, k % STAGES, e0 * F:(e0 + PIECE) * F].rearrange("d (e f) -> d e f", f=F),
                            up_v[:, i * 2 * PIECE + e0:i * 2 * PIECE + e0 + PIECE, :]).then_inc(piece_in[k], 16)
                else:
                    for c0 in range(0, PIECE, PIECE // 2):
                        sync.dma_start(
                            stage[:, k % STAGES, c0 * P:(c0 + PIECE // 2) * P].rearrange("p (c d) -> p c d", d=D),
                            down_v[:, i * PIECE + c0:i * PIECE + c0 + PIECE // 2, :]).then_inc(piece_in[k], 16)
                if k >= 1 and k < G:
                    sync.dma_start(x_sb[:, k], x_v[k]).then_inc(x_in[k], 16)
            with sync.Fori(0, G) as g:
                sync.wait_ge(out_ready, g + 2)
                sync.dma_start(out_v[bass.ds(g, 1)].rearrange("o p t d -> (o p) t d"), out_sb[:]).then_inc(out_done, 16)
            sync.wait_ge(out_done, 16 * (G + 1))

        @block.gpsimd
        def _(pool):
            nc.gpsimd.memset(ident[:], 0.0).then_inc(pool_own, 1)
            pool.wait_ge(pool_own, 1)
            nc.gpsimd.affine_select(out=ident[:], in_=ident[:], compare_op=ALU.not_equal, fill=1.0, base=0,
                                    pattern=[[-1, P]], channel_multiplier=1).then_inc(ident_done, 1)
            nc.gpsimd.memset(minus_one[:], -1.0).then_inc(ident_done, 1)
            nc.gpsimd.memset(zeros[:], 0.0).then_inc(ident_done, 1)

            def state_out(g):
                pool.wait_ge(sum_done, g + 1)
                nc.gpsimd.tensor_tensor(s_sum[:], s_sum[:], Ct[:], ALU.mult).then_inc(ss_done, 1)
                pool.wait_ge(ss_done, g + 1)
                nc.gpsimd.tensor_tensor(y_sb[:], s_sum[:], Ct[:], ALU.mult).then_inc(y_done, 1)

            pool.wait_ge(mod_done, 1)
            gates = mod[:, GA:GB + 1:GB - GA]
            nc.gpsimd.tensor_scalar(gate_sign[:], gates, 0.0, 2.0, ALU.is_ge, ALU.mult).then_inc(pool_own, 1)
            pool.wait_ge(pool_own, 2)
            nc.gpsimd.tensor_scalar(gate_sign[:], gate_sign[:], -1.0, None, ALU.add).then_inc(pool_own, 1)
            pool.wait_ge(pool_own, 3)
            nc.gpsimd.tensor_tensor(gate_size[:], gates, gate_sign[:], ALU.mult).then_inc(pool_own, 1)
            pool.wait_ge(pool_own, 4)
            nc.gpsimd.tensor_scalar(gate_size[:], gate_size[:], 0.25, None, ALU.max).then_inc(pool_own, 1)
            pool.wait_ge(pool_own, 5)
            nc.gpsimd.tensor_tensor(gates, gate_size[:], gate_sign[:], ALU.mult).then_inc(pool_own, 1)
            pool.wait_ge(pool_own, 6)
            pool.wait_ge(vec_in, 16 * 4)
            nc.gpsimd.tensor_scalar(mod[:, BOGA], mod[:, GA], bo_sb[:, 0:1], None, ALU.mult).then_inc(gates_done, 1)

            for k in range(2 * NP + 1):
                pool.wait_ge(w_hi, 2 * (k + 1) if k == 0 else k + 2)
                if k == 0:
                    nc.gpsimd.tensor_tensor(up_lo[:, 0, :], shared_raw[:, 0, :], up_hi[:, 0, :].bitcast(fp32),
                                            ALU.subtract)
                    nc.gpsimd.tensor_tensor(down_lo[:, 0, :], shared_raw[:, 1, :], down_hi[:, 0, :].bitcast(fp32),
                                            ALU.subtract).then_inc(w_lo, 1)
                else:
                    lo, hi = (up_lo, up_hi) if (k - 1) % 2 == 0 else (down_lo, down_hi)
                    c0 = 1 + (k - 1) // 2 * PIECE
                    nc.gpsimd.tensor_tensor(
                        lo[:, c0:c0 + PIECE, :],
                        stage[:, (k - 1) % STAGES].rearrange("p (c m) -> p c m", m=P),
                        hi[:, c0:c0 + PIECE, :].bitcast(fp32), ALU.subtract).then_inc(w_lo, 1)

            def lo_part(g, ch):
                if ch == 0:
                    return
                pool.wait_ge(hi_done, chunks(g, ch))
                nc.gpsimd.tensor_tensor(g_lo[:, ch % RING], g_ring[:, ch % RING],
                                        g_hi[:, ch % RING].bitcast(fp32), ALU.subtract).then_inc(lo_done, 1)

            pool.wait_ge(h2hi_done, 1)
            nc.gpsimd.tensor_tensor(h2_lo[:], h2T[:], h2_hi[:].bitcast(fp32), ALU.subtract).then_inc(h2lo_done, 1)
            for ch in range(PARTS):
                lo_part(0, ch)

            def turn(g, state_out_step=POOL_STATE_OUT, last=False):
                for j in range(TURN, NC + TURN):
                    lo_part(*at(g, j + PARTS))
                    if not last and j == state_out_step:
                        state_out(g + 2)

            for j in range(TURN):
                lo_part(0, j + PARTS)
            turn(0, POOL_STATE_OUT_0)
            with pool.Fori(1, G - 2) as g:
                turn(g)
            turn(G - 2, last=True)
            for j in range(TURN, NC - PARTS):
                lo_part(G - 1, j + PARTS)

        @block.scalar
        def _(act):
            def mod_of(row, g, half):
                return mod[:, row, bass.ds(2 * g + half, 1)]

            def modulate(dst, src, scale_row, bias_row, g, done):
                for half in range(2):
                    cols = slice(half * S, (half + 1) * S)
                    nc.scalar.activation(dst[:, cols], src[half][:, cols], ACT.Identity,
                                         scale=mod_of(scale_row, g, half), bias=mod_of(bias_row, g, half)).then_inc(done, 1)

            def norm1(g, bank=T_ps):
                act.wait_ge(xn1_ps, g + 1)
                modulate(h1T, (bank, bank), CA, SA, g, h1_done)

            def step_size(g, bank=T_ps):
                act.wait_ge(d_ps, g + 1)
                nc.scalar.activation(sp[:, 1], bank[:, 0:TL], ACT.Abs, bias=bd_sb[:, 0:1]).then_inc(z_done, 1)
                nc.scalar.activation(sp[:, 0], bank[:, 0:TL], ACT.Identity, bias=bd_sb[:, 0:1])
                act.wait_ge(z_done, g + 1)
                nc.scalar.activation(sp[:, 2], sp[:, 1], ACT.Silu, scale=-1.0,
                                     bias=minus_one[:, 0:1]).then_inc(sps_done, 1)

            def gate1(g):
                act.wait_ge(y_ps, g + 1)
                modulate(uT, (Q_ps, T_ps), GA, BOGA, g, u_done)

            def norm2(g):
                act.wait_ge(xn2_ps, g + 1)
                modulate(h2T, (T_ps, T_ps), CB, SB, g, h2_done)

            def router(g):
                act.wait_ge(aff_ps, g + 1)
                q = Q_ps[:, 0:TL * E].rearrange("p (t e) -> p t e", e=E)
                nc.scalar.activation(aff[:], q, ACT.Copy).then_inc(aff_done, 1)
                nc.scalar.activation(az[:], q, ACT.Abs).then_inc(az_done, 1)
                act.wait_ge(az_done, g + 1)
                nc.scalar.activation(sz[:], az[:], ACT.Silu, scale=-1.0, bias=minus_one[:, 0:1]).then_inc(sz_done, 1)

            def hand_over_tokens(g):
                act.wait_ge(h2_done, 2 * g + 2)
                need(act, tokens_read, g)
                nc.scalar.copy(h2_hi[:], h2T[:]).then_inc(h2hi_done, 1)

            def hand_over_weights(g):
                act.wait_ge(cwT_ps, g + 1)
                need(act, bc_done, routed(g - 1, NR))
                nc.scalar.copy(cw_T[:], T_ps[:]).then_inc(cwT_done, 1)

            def silu_part(g, ch):
                act.wait_ge(up_done, chunks(g, ch))
                if ch == 0:
                    need(act, lo_done, routed(g - 1, NC - RING))
                    nc.scalar.activation(g_ring[:, 0], up_ps[0][:], ACT.Silu).then_inc(s_done, 1)
                else:
                    need(act, g_done, routed(g, ch - RING) if ch > RING else routed(g - 1, NC - RING + ch % RING))
                    nc.scalar.activation(s_ring[:, ch % RING], up_ps[ch % RING][:], ACT.Silu).then_inc(s_done, 1)

            def hi_part(g, ch):
                if ch == 0:
                    act.wait_ge(s_done, chunks(g, ch))
                else:
                    act.wait_ge(g_done, routed(g, ch))
                need(act, down_done, chunks(g, ch - RING))
                nc.scalar.copy(g_hi[:, ch % RING], g_ring[:, ch % RING]).then_inc(hi_done, 1)

            def step(g, j):
                hi_part(*at(g, j + PARTS))
                silu_part(*at(g, j + UP))

            def finish(g):
                act.wait_ge(down_done, chunks(g, NC - 1))
                for half in range(2):
                    cols = slice(half * S, (half + 1) * S)
                    last = nc.scalar.activation(fT[:, cols], down_ps[:, cols], ACT.Copy, scale=mod_of(GB, g, half))
                last.then_inc(f_done, 1)

            act.wait_ge(c_in, 16)
            nc.scalar.activation(cs_sb[:], c_sb[:], ACT.Silu).then_inc(cs_done, 1)
            act.wait_ge(both_done, 1)
            nc.scalar.copy(sel[:], both[:].unsqueeze(2).broadcast_to([P, E, F])).then_inc(sel_done, 1)

            def split(k):
                act.wait_ge(piece_in[k], 32)
                hi = up_hi if k % 2 == 0 else down_hi
                c0 = 1 + k // 2 * PIECE
                nc.scalar.copy(hi[:, c0:c0 + PIECE, :],
                               stage[:, k % STAGES].rearrange("p (c m) -> p c m", m=P)).then_inc(w_hi, 1)

            act.wait_ge(mod_done, 1)
            norm1(0)
            act.wait_ge(shared_in, 64)
            nc.scalar.copy(up_hi[:, 0, :], shared_raw[:, 0, :]).then_inc(w_hi, 1)
            nc.scalar.copy(down_hi[:, 0, :], shared_raw[:, 1, :]).then_inc(w_hi, 1)
            act.wait_ge(bd_in, 16)
            step_size(0, up_ps[2])
            act.wait_ge(wT_ps, 2)
            nc.scalar.copy(Wo_T[:], up_ps[1][:, 0:D])
            nc.scalar.copy(cent_T[:], up_ps[1][:, D:D + E]).then_inc(wT_done, 1)
            for k in range(2 * NP - 2):
                split(k)
            act.wait_ge(gates_done, 1)
            gate1(0)
            act.wait_ge(ln1_done, 2)
            for t in range(TL):
                nc.scalar.activation(xn1[:, t], x_sb[:, 1, t], ACT.Identity, scale=ln1[:, 0, 1, t:t + 1],
                                     bias=ln1[:, 1, 1, t:t + 1]).then_inc(xn1_done, 1)
            split(2 * NP - 2)
            norm1(1, up_ps[0])
            split(2 * NP - 1)
            step_size(1, up_ps[2])
            norm2(0)
            router(0)
            hand_over_tokens(0)
            for ch in range(PARTS):
                silu_part(0, ch)
            silu_part(0, PARTS)
            hi_part(0, 0)
            hand_over_weights(0)
            for ch in range(PARTS + 1, LAG):
                silu_part(0, ch)
                hi_part(0, ch - PARTS)

            def turn(g, following=ACT_NEXT, ahead=ACT_AHEAD, last=False):
                for j in range(TURN, NC + TURN):
                    if j == NC - UP - 1:
                        hand_over_tokens(g + 1)
                    step(g, j)
                    if j == following["gate1"]:
                        gate1(g + 1)
                    if j == following["norm2"]:
                        norm2(g + 1)
                    if j == following["router"]:
                        router(g + 1)
                    if j == following["hand_over_weights"]:
                        hand_over_weights(g + 1)
                    if not last and j == ahead["norm1"]:
                        norm1(g + 2)
                    if not last and j == ahead["step_size"]:
                        step_size(g + 2)
                    if j == ACT_FINISH:
                        finish(g)

            for j in range(TURN):
                step(0, j)
            turn(0, ACT_NEXT_0, ACT_AHEAD_0)
            with act.Fori(1, G - 2) as g:
                turn(g)
            turn(G - 2, last=True)
            for j in range(TURN, NC - UP):
                step(G - 1, j)
            for j in range(NC - UP, NC - PARTS):
                hi_part(G - 1, j + PARTS)
            finish(G - 1)

        @block.vector
        def _(dve):
            DVE_LINKS = 57
            chain = {"base": 0, "n": 0}

            def link(ins):
                chain["n"] += 1
                ins.then_inc(dve_own, 1)
                dve.wait_ge(dve_own, chain["base"] + chain["n"])

            def settle():
                dve.wait_ge(dve_own, chain["base"] + chain["n"])

            def mark(ins):
                chain["n"] += 1
                ins.then_inc(dve_own, 1)

            def atanh_of(t, p, s):
                link(nc.vector.tensor_tensor(t, s, s, ALU.mult))
                link(nc.vector.tensor_scalar(p, t, ATANH_D[3], None, ALU.mult))
                for k in (2, 1, 0):
                    link(nc.vector.scalar_tensor_tensor(p, p, ATANH_D[k], t, ALU.add, ALU.mult))
                link(nc.vector.scalar_tensor_tensor(p, p, 1.0, s, ALU.add, ALU.mult))

            def rsqrt_guess(y, v, var):
                link(nc.vector.tensor_scalar(v, var, LN_EPS, None, ALU.add))
                link(nc.vector.tensor_scalar(y.bitcast(i32), v.bitcast(i32), -0.5, RSQRT_GUESS, ALU.mult, ALU.add))

            def rsqrt_step(y, v, a):
                link(nc.vector.tensor_tensor(a, y, y, ALU.mult))
                link(nc.vector.scalar_tensor_tensor(a, a, -0.5, v, ALU.mult, ALU.mult))
                link(nc.vector.scalar_tensor_tensor(y, a, 1.5, y, ALU.add, ALU.mult))

            def deviations(mean, var, v, a, out):
                y = out[0]
                rsqrt_guess(y, v, var)
                for step in range(RSQRT_STEPS):
                    rsqrt_step(y, v, a)
                return nc.vector.scalar_tensor_tensor(out[1], mean, -1.0, y, ALU.mult, ALU.mult)

            def stats_of(g, t):
                return nc.vector.bn_stats(stats1[:, t], x_sb[:, g, t])

            def aggregate(g):
                settle()
                nc.vector.memset(pad[:], 0.0)
                for t in range(TL):
                    last = nc.vector.bn_aggr(mv1[:, g, t], stats1[:, t])
                mark(last)

            def moments(g, dst, stats=stats):
                for t in range(TL):
                    last = nc.vector.bn_stats(stats[:, t], x_sb[:, g, t])
                link(last)
                nc.vector.memset(pad[:], 0.0)
                for t in range(TL):
                    last = nc.vector.bn_aggr(dst[:, t], stats[:, t])
                return last

            def step_size_a(g):
                dve.wait_ge(sps_done, g + 1)
                dve.wait_ge(z_done, g + 1)
                nc.vector.tensor_scalar(sp[:, 3], sp[:, 0], 0.0, None, ALU.max)
                link(nc.vector.scalar_tensor_tensor(sp[:, 4], sp[:, 1], 1.0, sp[:, 2], ALU.add, ALU.add))
                link(nc.vector.scalar_tensor_tensor(sp[:, 4], sp[:, 2], -EULER / 2, sp[:, 4], ALU.mult, ALU.add))
                link(nc.vector.reciprocal(sp[:, 4], sp[:, 4]))
                mark(nc.vector.scalar_tensor_tensor(sp[:, 6], sp[:, 2], -EULER / 2, sp[:, 4], ALU.mult, ALU.mult))

            def step_size_b(g):
                settle()
                link(nc.vector.tensor_tensor(sp[:, 7], sp[:, 6], sp[:, 6], ALU.mult))
                link(nc.vector.tensor_scalar(sp[:, 4], sp[:, 7], ATANH_D[3], None, ALU.mult))
                mark(nc.vector.scalar_tensor_tensor(sp[:, 4], sp[:, 4], ATANH_D[2], sp[:, 7], ALU.add, ALU.mult))

            def step_size_c(g):
                settle()
                for k in (1, 0):
                    link(nc.vector.scalar_tensor_tensor(sp[:, 4], sp[:, 4], ATANH_D[k], sp[:, 7], ALU.add, ALU.mult))
                link(nc.vector.scalar_tensor_tensor(sp[:, 4], sp[:, 4], 1.0, sp[:, 6], ALU.add, ALU.mult))
                nc.vector.scalar_tensor_tensor(
                    delta_b[:], sp[:, 4].unsqueeze(2).broadcast_to([P, TL, N]), 2.0,
                    sp[:, 3].unsqueeze(2).broadcast_to([P, TL, N]), ALU.mult, ALU.add).then_inc(delta_done, 1)

            def decay_a(g):
                dve.wait_ge(delta_ps, g + 1)
                link(nc.vector.tensor_scalar(u_sb[:], Q_ps[:, S:2 * S], A_sb[:, 0:1], U_LEAST, ALU.mult, ALU.max))
                link(nc.vector.tensor_scalar(n_sb[:], u_sb[:], LOG2E, MAGIC, ALU.mult, ALU.add))
                mark(nc.vector.tensor_scalar(n_sb[:], n_sb[:], -MAGIC, None, ALU.add))

            def decay_b(g):
                settle()
                mark(nc.vector.scalar_tensor_tensor(u_sb[:], n_sb[:], -LN2, u_sb[:], ALU.mult, ALU.add))
                nc.vector.tensor_scalar(pow2[:], n_sb[:], MANT, 127 * MANT, ALU.mult, ALU.add)
                settle()
                link(nc.vector.tensor_scalar(p_sb[:], u_sb[:], EXP_C[4], EXP_C[3], ALU.mult, ALU.add))
                mark(nc.vector.tensor_tensor(p_sb[:], p_sb[:], u_sb[:], ALU.mult))

            def decay_c1(g):
                settle()
                mark(nc.vector.scalar_tensor_tensor(p_sb[:], p_sb[:], EXP_C[2], u_sb[:], ALU.add, ALU.mult))

            def decay_c2(g):
                settle()
                link(nc.vector.scalar_tensor_tensor(p_sb[:], p_sb[:], EXP_C[1], u_sb[:], ALU.add, ALU.mult))
                mark(nc.vector.scalar_tensor_tensor(p_sb[:], p_sb[:], EXP_C[0], u_sb[:], ALU.add, ALU.mult))

            def decay_d1(g):
                settle()
                link(nc.vector.scalar_tensor_tensor(p_sb[:], p_sb[:], 1.0, u_sb[:], ALU.add, ALU.mult))
                mark(nc.vector.scalar_tensor_tensor(dA[:], p_sb[:], 1.0, pow2[:].bitcast(fp32), ALU.add, ALU.mult))

            def decay_d2(g):
                settle()
                nc.vector.memset(Ct[:, 0:1], 1.0)
                mark(nc.vector.tensor_tensor_scan(Ct[:, 1:S], dA[:, 0:S - 1], zeros[:, 0:S - 1], 1.0,
                                                  ALU.mult, ALU.add))

            def state_a(g):
                dve.wait_ge(b_ps, g + 1)
                nc.vector.tensor_scalar(p_sb[:], dA[:], -1.0, rA[:, 0:1], ALU.add, ALU.mult)
                settle()
                mark(nc.vector.tensor_scalar(u_sb[:], Ct[:], SSM_EPS, None, ALU.add))
                settle()
                mark(nc.vector.scalar_tensor_tensor(dB[:], Q_ps[:, 0:S], bB_sb[:, 0:1], p_sb[:], ALU.add, ALU.mult))

            def state_b1(g):
                settle()
                mark(nc.vector.reciprocal(u_sb[:, 0:S // 2], u_sb[:, 0:S // 2]))

            def state_b2(g):
                mark(nc.vector.reciprocal(u_sb[:, S // 2:S], u_sb[:, S // 2:S]))

            def state_c(g):
                settle()
                link(nc.vector.tensor_tensor(dB[:], dB[:], u_sb[:], ALU.mult))
                nc.vector.tensor_tensor_scan(s_sum[:], dB[:], zeros[:], 0.0, ALU.add, ALU.add).then_inc(sum_done, 1)

            def state_out(g):
                dve.wait_ge(sum_done, g + 1)
                nc.vector.tensor_tensor(s_sum[:], s_sum[:], Ct[:], ALU.mult).then_inc(ss_done, 1)
                dve.wait_ge(ss_done, g + 1)
                nc.vector.tensor_tensor(y_sb[:], s_sum[:], Ct[:], ALU.mult).then_inc(y_done, 1)

            def residual1(g):
                dve.wait_ge(u_ps, g + 1)
                mark(nc.vector.tensor_tensor(x_sb[:, g].rearrange("p t d -> p (t d)"),
                                             x_sb[:, g].rearrange("p t d -> p (t d)"), Q_ps[:], ALU.add))

            def moments2_a(g):
                settle()
                nc.vector.memset(pad[:], 0.0)
                for t in range(TL):
                    last = nc.vector.bn_stats(stats[:, t], x_sb[:, g, t])
                mark(last)

            def moments2_b(g):
                settle()
                nc.vector.memset(pad[:], 0.0)
                for t in range(TL):
                    last = nc.vector.bn_aggr(mv[:, t], stats[:, t])
                mark(last)

            def deviations2_a(g):
                settle()
                rsqrt_guess(ln2[:, 0], rs[:, 0], mv[:, :, 1])
                rsqrt_step(ln2[:, 0], rs[:, 0], rs[:, 1])

            def deviations2_b(g):
                rsqrt_step(ln2[:, 0], rs[:, 0], rs[:, 1])

            def deviations2_c(g):
                rsqrt_step(ln2[:, 0], rs[:, 0], rs[:, 1])
                mark(nc.vector.scalar_tensor_tensor(ln2[:, 1], mv[:, :, 0], -1.0, ln2[:, 0], ALU.mult, ALU.mult))

            def normalise1(g):
                settle()
                for t in range(TL):
                    nc.vector.tensor_scalar(xn1[:, t], x_sb[:, g, t], ln1[:, 0, g, t:t + 1], ln1[:, 1, g, t:t + 1],
                                            ALU.mult, ALU.add).then_inc(xn1_done, 1)

            def normalise2(g):
                settle()
                for t in range(TL):
                    nc.vector.tensor_scalar(xn2[:, t], x_sb[:, g, t], ln2[:, 0, t:t + 1], ln2[:, 1, t:t + 1],
                                            ALU.mult, ALU.add).then_inc(xn2_done, 1)

            def router_top(g):
                dve.wait_ge(aff_done, g + 1)
                link(nc.vector.tensor_tensor(biased[:], aff[:], bias_sb[:].unsqueeze(1).broadcast_to([P, TL, E]), ALU.add))
                nc.vector.memset(pad[:], 0.0)
                for t in range(TL):
                    last = nc.vector.max(top[:, t], biased[:, t])
                mark(last)

            def router_chosen(g):
                settle()
                nc.vector.memset(pad[:], 0.0)
                for t in range(TL):
                    last = nc.vector.match_replace(left[:, t], top[:, t], biased[:, t], LOWEST)
                mark(last)

            def sigmoid_a(g):
                dve.wait_ge(sz_done, g + 1)
                dve.wait_ge(az_done, g + 1)
                link(nc.vector.scalar_tensor_tensor(az[:], az[:], 1.0, sz[:], ALU.add, ALU.add))
                mark(nc.vector.scalar_tensor_tensor(aff[:], aff[:], 0.0, az[:], ALU.is_ge, ALU.mult))

            def sigmoid_b(g):
                nc.vector.scalar_tensor_tensor(ez[:], sz[:], -EULER, az[:], ALU.mult, ALU.add)
                settle()
                mark(nc.vector.scalar_tensor_tensor(aff[:], sz[:], -EULER, aff[:], ALU.mult, ALU.max))

            def sigmoid_over1(g):
                settle()
                mark(nc.vector.reciprocal(ez[:, 0:TL // 2], ez[:, 0:TL // 2]))

            def sigmoid_over2(g):
                mark(nc.vector.reciprocal(ez[:, TL // 2:TL], ez[:, TL // 2:TL]))

            def router_sum(g):
                settle()
                link(nc.vector.scalar_tensor_tensor(aff[:], left[:], LOWEST, aff[:], ALU.is_equal, ALU.mult))
                link(nc.vector.tensor_tensor(ez[:], aff[:], ez[:], ALU.mult))
                mark(nc.vector.tensor_reduce(wsum[:], ez[:], AX.X, ALU.add))

            def router_scale(g):
                settle()
                link(nc.vector.tensor_scalar(wsum[:], wsum[:], SUM_EPS, None, ALU.add))
                link(nc.vector.reciprocal(wsum[:], wsum[:]))
                mark(nc.vector.tensor_tensor(ez[:], ez[:], wsum[:].unsqueeze(2).broadcast_to([P, TL, E]), ALU.mult))

            def router_split(g):
                settle()
                link(nc.vector.tensor_copy(cw_hl[:, :, 0], ez[:]))
                nc.vector.tensor_tensor(cw_hl[:, :, 1], ez[:], cw_hl[:, :, 0].bitcast(fp32),
                                        ALU.subtract).then_inc(cw_done, 1)

            def hand_over(g):
                dve.wait_ge(h2hi_done, g + 1)
                need(dve, up_done, chunks(g - 1, NC - 1))
                nc.vector.tensor_tensor(h2_lo[:], h2T[:], h2_hi[:].bitcast(fp32), ALU.subtract).then_inc(h2lo_done, 1)

            def weigh(g, ch):
                if ch == 0:
                    return
                dve.wait_ge(s_done, chunks(g, ch))
                dve.wait_ge(bc_done, routed(g, ch))
                if ch == RING:
                    dve.wait_ge(shared_lo_done, g + 1)
                else:
                    need(dve, lo_done, routed(g, ch - RING) if ch > RING else routed(g - 1, NC - RING + ch))
                nc.vector.tensor_tensor(g_ring[:, ch % RING], s_ring[:, ch % RING], cw_ps[ch % 2][:],
                                        ALU.mult).then_inc(g_done, 1)

            def shared_lo(g):
                dve.wait_ge(hi_done, chunks(g, 0))
                rows = slice(F, 2 * F)
                nc.vector.tensor_tensor(g_hi[rows, 0], g_ring[rows, 0], g_hi[rows, 0].bitcast(fp32),
                                        ALU.subtract).then_inc(shared_lo_done, 1)

            def finish(g):
                dve.wait_ge(f_ps, g + 1)
                dve.wait_ge(out_done, 16 * (g + 1))
                nc.vector.tensor_tensor(out_sb[:].rearrange("p t d -> p (t d)"),
                                        x_sb[:, g].rearrange("p t d -> p (t d)"), T_ps[:], ALU.add).then_inc(out_ready, 1)

            def W(i):
                return wk[:, i:i + 1]

            def rate_a():
                LN2_HI, LN2_LO = 0.693359375, -2.12194440e-4
                link(nc.vector.scalar_tensor_tensor(W(1), W(0), -1.0, W(0), ALU.mult, ALU.max))
                link(nc.vector.tensor_scalar(W(1), W(1), -U_LEAST, None, ALU.min))
                link(nc.vector.tensor_scalar(W(2), W(1), LOG2E, MAGIC, ALU.mult, ALU.add))
                link(nc.vector.tensor_scalar(W(2), W(2), -MAGIC, None, ALU.add))
                link(nc.vector.scalar_tensor_tensor(W(3), W(2), -LN2_HI, W(1), ALU.mult, ALU.add))
                link(nc.vector.scalar_tensor_tensor(W(3), W(2), -LN2_LO, W(3), ALU.mult, ALU.add))
                link(nc.vector.tensor_scalar(W(3), W(3), -1.0, None, ALU.mult))
                link(nc.vector.tensor_scalar(W(4), W(3), EXP_C[4], EXP_C[3], ALU.mult, ALU.add))

            def rate_b():
                link(nc.vector.tensor_tensor(W(4), W(4), W(3), ALU.mult))
                for add in (EXP_C[2], EXP_C[1], EXP_C[0], 1.0):
                    link(nc.vector.scalar_tensor_tensor(W(4), W(4), add, W(3), ALU.add, ALU.mult))
                link(nc.vector.tensor_scalar(wki[:], W(2), -MANT, 127 * MANT, ALU.mult, ALU.add))
                link(nc.vector.scalar_tensor_tensor(W(5), W(4), 1.0, wki[:].bitcast(fp32), ALU.add, ALU.mult))
                link(nc.vector.tensor_scalar(W(7), W(5), 2.0, None, ALU.add))
                link(nc.vector.reciprocal(W(7), W(7)))
                link(nc.vector.tensor_tensor(W(8), W(5), W(7), ALU.mult))

            def rate_c():
                atanh_of(W(9), W(10), W(8))
                link(nc.vector.tensor_scalar(W(6), W(0), 0.0, -1.0, ALU.max, ALU.mult))
                link(nc.vector.scalar_tensor_tensor(A_sb[:], W(10), -2.0, W(6), ALU.mult, ALU.add))
                link(nc.vector.tensor_scalar(rA[:], A_sb[:], SSM_EPS, None, ALU.add))
                link(nc.vector.reciprocal(rA[:], rA[:]))

            dve.sem_inc(out_ready, 1)
            dve.wait_ge(ident_done, 3)
            nc.vector.tensor_tensor(both[:], ident[:, 0:E], ident[:, E:2 * E], ALU.add).then_inc(both_done, 1)
            dve.wait_ge(x_in[0], 16)
            dve.wait_ge(csT_ps, 1)
            nc.vector.tensor_copy(cs_T[:], Q_ps[:, 0:BATCH]).then_inc(csT_done, 1)
            link(moments(0, mv1[:, 0]))
            deviations(mv1[:, 0, :, 0], mv1[:, 0, :, 1], rs1[:, 0, 0], rs1[:, 1, 0],
                       (ln1[:, 0, 0], ln1[:, 1, 0])).then_inc(ln1_done, 1)
            dve.wait_ge(ln1_done, 1)
            normalise1(0)
            dve.wait_ge(wT_ps, 1)
            nc.vector.tensor_copy(WB_T[:], up_ps[0][:, 0:N]).then_inc(wT_done, 1)
            dve.wait_ge(mod_ps, 1)
            m = Q_ps[:, 0:6 * BATCH].rearrange("p (r b) -> p r b", b=BATCH)
            link(nc.vector.tensor_copy(mod[:, 0:6], m))
            for r in (CA, CB):
                last = nc.vector.tensor_scalar(mod[:, r], mod[:, r], 1.0, None, ALU.add)
            last.then_inc(mod_done, 1)
            dve.wait_ge(A_in, 32)
            rate_a()
            rate_b()
            step_size_a(0)
            step_size_b(0)
            step_size_c(0)
            rate_c()
            decay_a(0)
            dve.wait_ge(x_in[1], 16)
            stats_of(1, 0)
            decay_b(0)
            stats_of(1, 1)
            decay_c1(0)
            stats_of(1, 2)
            decay_c2(0)
            mark(stats_of(1, 3))
            decay_d1(0)
            aggregate(1)
            decay_d2(0)
            dve.wait_ge(vec_in, 16 * 4)
            state_a(0)
            dve.wait_ge(x_in[2], 16)
            stats_of(2, 0)
            state_b1(0)
            state_b2(0)
            stats_of(2, 1)
            state_c(0)
            stats_of(2, 2)
            state_out(0)
            mark(stats_of(2, 3))
            aggregate(2)
            settle()
            deviations(mv1[:, 1:3, :, 0], mv1[:, 1:3, :, 1], rs1[:, 0, 1:3], rs1[:, 1, 1:3],
                       (ln1[:, 0, 1:3], ln1[:, 1, 1:3])).then_inc(ln1_done, 1)
            dve.wait_ge(x_in[3], 16)
            for t in range(TL):
                last = stats_of(3, t)
            mark(last)
            residual1(0)
            moments2_a(0)
            moments2_b(0)
            deviations2_a(0)
            deviations2_b(0)
            deviations2_c(0)
            normalise2(0)
            aggregate(3)
            step_size_a(1)
            step_size_b(1)
            step_size_c(1)
            dve.wait_ge(x_in[4], 16)
            link(moments(4, mv1[:, 4], stats1))
            router_top(0)
            router_chosen(0)
            sigmoid_a(0)
            sigmoid_b(0)
            sigmoid_over1(0)
            sigmoid_over2(0)
            router_sum(0)
            router_scale(0)
            router_split(0)

            def turn(g, following=DVE_NEXT, ahead=DVE_AHEAD, moments_1={}, last=False):
                for j in range(TURN, NC + TURN):
                    weigh(*at(g, j + WEIGH))
                    if j == NC - PARTS:
                        shared_lo(g + 1)
                    if j == following["residual1"]:
                        residual1(g + 1)
                    if j == following["moments2_a"]:
                        moments2_a(g + 1)
                    if j == following["moments2_b"]:
                        moments2_b(g + 1)
                    if j == following["deviations2_a"]:
                        deviations2_a(g + 1)
                    if j == following["deviations2_b"]:
                        deviations2_b(g + 1)
                    if j == following["deviations2_c"]:
                        deviations2_c(g + 1)
                    if j == following["normalise2"]:
                        normalise2(g + 1)
                    if j == following["router_top"]:
                        router_top(g + 1)
                    if j == following["router_chosen"]:
                        router_chosen(g + 1)
                    if j == following["sigmoid_a"]:
                        sigmoid_a(g + 1)
                    if j == following["sigmoid_b"]:
                        sigmoid_b(g + 1)
                    if j == following["sigmoid_over1"]:
                        sigmoid_over1(g + 1)
                    if j == following["sigmoid_over2"]:
                        sigmoid_over2(g + 1)
                    if j == following["router_sum"]:
                        router_sum(g + 1)
                    if j == following["router_scale"]:
                        router_scale(g + 1)
                    if j == following["router_split"]:
                        router_split(g + 1)
                    if j == following["hand_over"]:
                        hand_over(g + 1)
                    if not last and j == ahead["normalise1"]:
                        normalise1(g + 2)
                    if not last and j == ahead["step_size_a"]:
                        step_size_a(g + 2)
                    if not last and j == ahead["step_size_b"]:
                        step_size_b(g + 2)
                    if not last and j == ahead["step_size_c"]:
                        step_size_c(g + 2)
                    if not last and j == ahead["decay_a"]:
                        decay_a(g + 2)
                    if not last and j == ahead["decay_b"]:
                        decay_b(g + 2)
                    if not last and j == ahead["decay_c1"]:
                        decay_c1(g + 2)
                    if not last and j == ahead["decay_c2"]:
                        decay_c2(g + 2)
                    if not last and j == ahead["decay_d1"]:
                        decay_d1(g + 2)
                    if not last and j == ahead["decay_d2"]:
                        decay_d2(g + 2)
                    if not last and j == ahead["state_a"]:
                        state_a(g + 2)
                    if not last and j == ahead["state_b1"]:
                        state_b1(g + 2)
                    if not last and j == ahead["state_b2"]:
                        state_b2(g + 2)
                    if not last and j == ahead["state_c"]:
                        state_c(g + 2)
                    for k in range(5, G):
                        if j == moments_1.get(f"moments{k}"):
                            link(moments(k, mv1[:, k], stats1))
                    if j == moments_1.get("deviations1"):
                        mark(deviations(mv1[:, 3:, :, 0], mv1[:, 3:, :, 1], rs1[:, 0, 3:], rs1[:, 1, 3:],
                                        (ln1[:, 0, 3:], ln1[:, 1, 3:])))
                    if j == DVE_FINISH:
                        finish(g)

            decay_a(1)
            shared_lo(0)
            decay_b(1)
            weigh(0, 1)
            decay_c1(1)
            weigh(0, 2)
            decay_c2(1)
            weigh(0, 3)
            decay_d1(1)
            decay_d2(1)
            state_a(1)
            weigh(0, 4)
            state_b1(1)
            state_b2(1)
            weigh(0, 5)
            state_c(1)
            state_out(1)
            for k in range(5, G):
                dve.wait_ge(x_in[k], 16)
            turn(0, DVE_NEXT_0, DVE_AHEAD_0, DVE_MOMENTS_0)
            setup_links = chain["n"]
            with dve.Fori(1, G - 2) as g:
                chain["base"], chain["n"] = (g - 1) * DVE_LINKS + setup_links, 0
                turn(g)
                assert chain["n"] == DVE_LINKS, chain["n"]
            chain["base"], chain["n"] = (G - 3) * DVE_LINKS + setup_links, 0
            turn(G - 2, last=True)
            for j in range(TURN, NC - WEIGH):
                weigh(G - 1, j + WEIGH)
            finish(G - 1)

        @block.tensor
        def _(pe):
            def tile_wait(done, per_group, g, t):
                if t * per_group % TL == 0:
                    pe.wait_ge(done, per_group * g + t * per_group // TL + 1)

            def transpose_tiles(dst, src, done, per_group, g):
                for t in range(TL):
                    tile_wait(done, per_group, g, t)
                    last = nc.tensor.transpose(dst[:, t * P:(t + 1) * P], src(t), ident[:])
                return last

            def norm1(g, bank=T_ps):
                transpose_tiles(bank, lambda t: xn1[:, t], xn1_done, TL, g).then_inc(xn1_ps, 1)

            def project_step(g, bank=T_ps):
                if bank is T_ps:
                    pe.wait_ge(h1_done, 2 * g + 2)
                for t in range(TL):
                    if bank is not T_ps:
                        tile_wait(h1_done, 2, g, t)
                    last = nc.tensor.matmul(bank[:, t:t + 1], h1T[:, t * P:(t + 1) * P], Wd_sb[:], start=True, stop=True)
                last.then_inc(d_ps, 1)

            def project_B(g):
                for half in range(2):
                    last = nc.tensor.matmul(Q_ps[half * N:(half + 1) * N, 0:S], WB_T[:],
                                            h1T[:, half * S:(half + 1) * S], start=True, stop=True)
                last.then_inc(b_ps, 1)

            def project(g):
                project_step(g)
                project_B(g)

            def spread(g):
                pe.wait_ge(delta_done, g + 1)
                for t in range(TL):
                    half, col = t // (TL // 2), S + t % (TL // 2) * P
                    last = nc.tensor.matmul(Q_ps[half * N:(half + 1) * N, col:col + P], delta_b[:, t], ident[:],
                                            start=True, stop=True)
                last.then_inc(delta_ps, 1)

            def state_out(g):
                pe.wait_ge(y_done, g + 1)
                need(pe, out_ready, g)
                for half in range(2):
                    rows = slice(half * N, (half + 1) * N)
                    last = nc.tensor.matmul((Q_ps, T_ps)[half][:, half * S:(half + 1) * S], Wo_T[rows, :], y_sb[rows, :],
                                            start=True, stop=True)
                last.then_inc(y_ps, 1)

            def residual1(g):
                transpose_tiles(Q_ps, lambda t: uT[:, t * P:(t + 1) * P], u_done, 2, g).then_inc(u_ps, 1)

            def norm2(g):
                transpose_tiles(T_ps, lambda t: xn2[:, t], xn2_done, TL, g).then_inc(xn2_ps, 1)

            def affinities(g):
                for t in range(TL):
                    tile_wait(h2_done, 2, g, t)
                    last = nc.tensor.matmul(Q_ps[:, t * E:(t + 1) * E], h2T[:, t * P:(t + 1) * P], cent_T[:],
                                            start=True, stop=True)
                last.then_inc(aff_ps, 1)

            def route(g, states=True):
                if states:
                    pe.wait_ge(sps_done, g + 2)
                transpose_tiles(T_ps, lambda t: cw_hl[:, t].rearrange("p h e -> p (h e)").bitcast(fp32),
                                cw_done, 1, g).then_inc(cwT_ps, 1)

            def up(g, ch, meanwhile=None):
                if ch == 0:
                    pe.wait_ge(h2hi_done, g + 1)
                    need(pe, s_done, chunks(g - 1, NC - RING))
                else:
                    need(pe, s_done, chunks(g, ch - RING))
                u = up_ps[ch % RING]
                nc.tensor.matmul(u[:], up_lo[:, ch, :], h2_hi[:], start=True, stop=False)
                if ch == 0:
                    nc.tensor.matmul(u[:], up_hi[:, ch, :], h2_hi[:], start=False, stop=False)
                    if meanwhile is not None:
                        meanwhile()
                    pe.wait_ge(h2lo_done, g + 1)
                    nc.tensor.matmul(u[:], up_hi[:, ch, :], h2_lo[:], start=False, stop=True).then_inc(up_done, 1)
                    return
                middle = nc.tensor.matmul(u[:], up_hi[:, ch, :], h2_hi[:], start=False, stop=False)
                if ch == NC - 1:
                    middle.then_inc(tokens_read, 1)
                nc.tensor.matmul(u[:], up_hi[:, ch, :], h2_lo[:], start=False, stop=True).then_inc(up_done, 1)

            def weights(g, ch):
                if ch == 0:
                    return
                if ch == 1:
                    pe.wait_ge(cwT_done, g + 1)
                need(pe, g_done, routed(g, ch - 2))
                nc.tensor.matmul(cw_ps[ch % 2][:], sel[:, 2 * ch - 2:2 * ch, :].rearrange("p e f -> p (e f)"), cw_T[:],
                                 start=True, stop=True).then_inc(bc_done, 1)

            def down(g, ch):
                if ch == 0:
                    need(pe, f_done, g)
                    pe.wait_ge(shared_lo_done, g + 1)
                    nc.tensor.matmul(down_ps[:], down_lo[:, 0, :], g_hi[:, 0], start=True, stop=False)
                    nc.tensor.matmul(down_ps[:], down_hi[:, 0, :], g_hi[:, 0], start=False, stop=False).then_inc(down_done, 1)
                    return
                pe.wait_ge(hi_done, chunks(g, ch))
                nc.tensor.matmul(down_ps[:], down_lo[:, ch, :], g_hi[:, ch % RING], start=False, stop=False)
                nc.tensor.matmul(down_ps[:], down_hi[:, ch, :], g_hi[:, ch % RING], start=False, stop=False)
                pe.wait_ge(lo_done, routed(g, ch))
                nc.tensor.matmul(down_ps[:], down_hi[:, ch, :], g_lo[:, ch % RING], start=False,
                                 stop=ch == NC - 1).then_inc(down_done, 1)

            def finish(g):
                transpose_tiles(T_ps, lambda t: fT[:, t * P:(t + 1) * P], f_done, 1, g).then_inc(f_ps, 1)

            pe.wait_ge(ident_done, 1)
            pe.wait_ge(cs_done, 1)
            nc.tensor.transpose(Q_ps[:, 0:BATCH], cs_sb[:], ident[0:BATCH, 0:BATCH]).then_inc(csT_ps, 1)
            pe.wait_ge(WB_in, 32)
            nc.tensor.transpose(up_ps[0][:, 0:N], WB_sb[:], ident[0:N, 0:N]).then_inc(wT_ps, 1)
            pe.wait_ge(csT_done, 1)
            pe.wait_ge(wmod_in, 16)
            for r in range(6):
                last = nc.tensor.matmul(Q_ps[:, r * BATCH:(r + 1) * BATCH], wmod_sb[:, r * D:(r + 1) * D], cs_T[:],
                                        start=True, stop=True)
            last.then_inc(mod_ps, 1)
            norm1(0)
            pe.wait_ge(wT_done, 1)
            project_step(0, up_ps[2])
            project_B(0)
            pe.wait_ge(Wo_in, 32)
            nc.tensor.transpose(up_ps[1][:, 0:D], Wo_sb[:].rearrange("d h n -> d (h n)"), ident[:])
            pe.wait_ge(cent_in, 16)
            nc.tensor.transpose(up_ps[1][:, D:D + E], cent_sb[:], ident[0:E, 0:E]).then_inc(wT_ps, 1)
            spread(0)
            pe.wait_ge(wT_done, 2)
            state_out(0)
            residual1(0)
            norm1(1, up_ps[0])
            project_step(1, up_ps[2])
            norm2(0)
            affinities(0)
            pe.wait_ge(w_lo, 2 * NP + 1)
            pe.wait_ge(sel_done, 1)
            pe.wait_ge(sps_done, 2)
            up(0, 0)
            pe.wait_ge(aff_done, 1)
            pe.wait_ge(az_done, 1)
            project_B(1)
            spread(1)
            up(0, 1)
            up(0, 2)
            route(0)
            weights(0, 1)
            up(0, 3)
            weights(0, 2)

            def turn(g, following=PE_NEXT, ahead=PE_AHEAD, last=False):
                for j in range(TURN, NC + TURN):
                    if j + UP == NC:
                        weights(*at(g, j + WEIGH))
                        up(*at(g, j + UP), meanwhile=lambda: down(g, j))
                    else:
                        up(*at(g, j + UP))
                        weights(*at(g, j + WEIGH))
                    if j == following["state_out"]:
                        state_out(g + 1)
                    if j == following["residual1"]:
                        residual1(g + 1)
                    if j == following["norm2"]:
                        norm2(g + 1)
                    if j == following["affinities"]:
                        affinities(g + 1)
                    if j == following["route"]:
                        route(g + 1, not last)
                    if not last and j == ahead["norm1"]:
                        norm1(g + 2)
                    if not last and j == ahead["project"]:
                        project(g + 2)
                    if not last and j == ahead["spread"]:
                        spread(g + 2)
                    if j == PE_FINISH:
                        finish(g)
                    if j + UP != NC:
                        down(*at(g, j))

            for j in range(TURN):
                up(0, j + UP)
                weights(0, j + WEIGH)
                down(0, j)
            turn(0, PE_NEXT_0, PE_AHEAD_0)
            with pe.Fori(1, G - 2) as g:
                turn(g)
            turn(G - 2, last=True)
            for j in range(TURN, NC - UP):
                up(G - 1, j + UP)
                weights(G - 1, j + WEIGH)
                down(G - 1, j)
            for j in range(NC - UP, NC):
                if j + WEIGH < NC:
                    weights(G - 1, j + WEIGH)
                down(G - 1, j)
            finish(G - 1)


_INS = ["L0_attn_x", "L0_attn_A_log", "L0_attn_WB", "L0_attn_bB", "L0_attn_Wd", "L0_attn_bd", "L0_attn_Wo",
        "L0_attn_bo", "L0_ffn_centroids", "L0_ffn_expert_biases", "L0_ffn_Ws_up", "L0_ffn_Ws_down",
        "L0_ffn_W_up", "L0_ffn_W_down", "L0_c", "L0_wmod"]


def kernel(**inputs):
    import numpy as _np
    import concourse.bacc as _bacc
    from concourse import mybir as _mybir
    from concourse.bass_utils import run_bass_kernel_spmd as _run

    nc = _bacc.Bacc("TRN2", target_bir_lowering=False, num_devices=1)
    arrays, args = {}, []
    for name in _INS:
        a = _np.ascontiguousarray(inputs[name])
        arrays[f"in_{name}"] = a
        args.append(nc.dram_tensor(f"in_{name}", a.shape, _mybir.dt.from_np(a.dtype), kind="ExternalInput").ap())
    shape = inputs["L0_attn_x"].shape
    args.append(nc.dram_tensor("out_0", shape, _mybir.dt.float32, kind="ExternalOutput").ap())
    adaln_ssm_moe_kernel(nc, *args)
    r = _run(nc, [arrays], core_ids=[0])
    return r.results[0]["out_0"]
```
